# Optimizing a Trainium2 kernel written in Bass

```python
import numpy as np
import jax
import jax.numpy as jnp

def _softmax(x, axis=-1):
    return jax.nn.softmax(x, axis=axis)

def _gelu(x):
    return jax.nn.gelu(x, approximate=True)

def _silu(x):
    return jax.nn.silu(x)

def _sigmoid(x):
    return jax.nn.sigmoid(x)

def _layernorm(x, axis=-1, eps=1e-05):
    m = jnp.mean(x, axis=axis, keepdims=True)
    v = jnp.var(x, axis=axis, keepdims=True)
    return (x - m) / jnp.sqrt(v + eps)

def _scatter_add(tgt, idx, src, axis=0):
    return tgt.at[idx].add(src)

def _segment_sum(src, seg, n):
    return jax.ops.segment_sum(src, seg, n)
kernel_name = 'mk_gnn_ffn_d2_gnn_r8_2027c5'

def setup_inputs(seed: int=0):
    np.random.seed(seed)
    _w = jnp.asarray

    def _rec_inputs():
        import jax
        import jax.numpy as jnp
        _gk = jax.random.key(seed)
        x = -0.0002117 + 1 * jax.random.normal(jax.random.fold_in(_gk, 1), (1250, 512), jnp.float32)
        _s = jax.random.randint(jax.random.fold_in(_gk, 2), (20000,), 0, 1250, jnp.int32)
        _d = jax.random.randint(jax.random.fold_in(_gk, 3), (20000,), 0, 1250, jnp.int32)
        _loop = jnp.arange(1250, dtype=jnp.int32)
        src = jnp.concatenate([_s, _d, _loop])
        dst = jnp.concatenate([_d, _s, _loop])
        _o = jnp.argsort(dst, stable=True)
        src = src[_o]
        dst = dst[_o]
        return (x, src, dst)
    x, src, dst = _rec_inputs()

    def _L0_gnn_setup():
        import jax, jax.numpy as jnp
        import numpy as np
        N = 6250
        IN_CH = 512
        OUT_CH = 512
        DEG = 32
        E = N * DEG
        key = jax.random.key(seed)
        kx, kwc, kwn, kb, ke = jax.random.split(key, 5)
        x = jax.random.normal(kx, (N, IN_CH), dtype=jnp.float32)
        bound = 1.0 / np.sqrt(IN_CH)
        wc = jax.random.uniform(kwc, (IN_CH, OUT_CH), minval=-bound, maxval=bound, dtype=jnp.float32)
        wn = jax.random.uniform(kwn, (IN_CH, OUT_CH), minval=-bound, maxval=bound, dtype=jnp.float32)
        bias = jax.random.uniform(kb, (OUT_CH,), minval=-bound, maxval=bound, dtype=jnp.float32)
        src = jnp.repeat(jnp.arange(N, dtype=jnp.int64), DEG)
        dst = jax.random.randint(ke, (E,), 0, N, dtype=jnp.int64)
        edge_index = jnp.stack([src, dst], axis=0)
        return {'x': x, 'wc': wc, 'wn': wn, 'bias': bias, 'edge_index': edge_index}
    _L0_gnn_all = _L0_gnn_setup()
    _L0_gnn_in = {k: v for k, v in _L0_gnn_all.items() if k in ('wc', 'wn', 'bias')}
    del _L0_gnn_all

    def _L0_ffn_setup():
        import jax, jax.numpy as jnp
        import numpy as np
        B, N, DIM = (1, 256, 512)
        DH, H = (64, 8)
        E, FF = (8, 256)

        def _layernorm(x, g, b, eps=1e-05):
            mu = jnp.mean(x, axis=-1, keepdims=True)
            var = jnp.mean(jnp.square(x - mu), axis=-1, keepdims=True)
            return (x - mu) * jax.lax.rsqrt(var + eps) * g + b

        def _l2norm(x, eps=1e-12):
            return x / jnp.sqrt(jnp.sum(jnp.square(x), axis=-1, keepdims=True) + eps)
        key = jax.random.key(seed)
        ks = jax.random.split(key, 12)
        g = lambda k, shape: jax.random.normal(k, shape, jnp.float32) * 0.02
        return {'x': jax.random.normal(ks[0], (B, N, DIM), jnp.float32), 'ln_g': jnp.ones((DIM,), jnp.float32), 'ln_b': jnp.zeros((DIM,), jnp.float32), 'Wq': g(ks[1], (DIM, DIM)), 'Wk': g(ks[2], (DIM, DIM)), 'Wv': g(ks[3], (DIM, DIM)), 'Wo': g(ks[4], (DIM, DIM)), 'qn_g': jnp.ones((DH,), jnp.float32), 'kn_g': jnp.ones((DH,), jnp.float32), 'gate_W': g(ks[5], (DIM, E)), 'gate_b': jnp.zeros((E,), jnp.float32), 'W1': g(ks[6], (E, DIM, FF)), 'b1': jnp.zeros((E, FF), jnp.float32), 'W2': g(ks[7], (E, FF, DIM)), 'b2': jnp.zeros((E, DIM), jnp.float32)}
    _L0_ffn_all = _L0_ffn_setup()
    _L0_ffn_in = {k: v for k, v in _L0_ffn_all.items() if k in ('ln_g', 'ln_b', 'Wq', 'Wk', 'Wv', 'Wo', 'qn_g', 'kn_g', 'gate_W', 'gate_b', 'W1', 'b1', 'W2', 'b2')}
    del _L0_ffn_all

    def _L1_gnn_setup():
        import jax, jax.numpy as jnp
        import numpy as np
        N_NODES = 1250
        N_EDGES = 20000
        IN_DIM = 512
        OUT_DIM = 512
        LN_EPS = 1e-05
        key = jax.random.key(seed)
        k_x, k_src, k_ws, k_wn = jax.random.split(key, 4)
        x = jax.random.normal(k_x, (N_NODES, IN_DIM), dtype=jnp.float32)
        edge_src = jax.random.randint(k_src, (N_EDGES,), 0, N_NODES, dtype=jnp.int32)
        edge_dst = jnp.repeat(jnp.arange(N_NODES, dtype=jnp.int32), N_EDGES // N_NODES)
        deg = jnp.full((N_NODES,), float(N_EDGES // N_NODES), dtype=jnp.float32)
        scale = 1.0 / np.sqrt(IN_DIM)
        W_self = jax.random.normal(k_ws, (OUT_DIM, IN_DIM), dtype=jnp.float32) * scale
        W_neigh = jax.random.normal(k_wn, (OUT_DIM, IN_DIM), dtype=jnp.float32) * scale
        bias = jnp.zeros((OUT_DIM,), dtype=jnp.float32)
        gamma = jnp.ones((OUT_DIM,), dtype=jnp.float32)
        beta = jnp.zeros((OUT_DIM,), dtype=jnp.float32)
        return {'x': x, 'edge_src': edge_src, 'edge_dst': edge_dst, 'deg': deg, 'W_self': W_self, 'W_neigh': W_neigh, 'bias': bias, 'gamma': gamma, 'beta': beta}
    _L1_gnn_all = _L1_gnn_setup()
    _L1_gnn_in = {k: v for k, v in _L1_gnn_all.items() if k in ('W_self', 'W_neigh', 'bias', 'gamma', 'beta')}
    del _L1_gnn_all

    def _L1_ffn_setup():
        import jax, jax.numpy as jnp
        import numpy as np
        from jax import lax
        N, M, DIM, HEADS, TOPK = (4, 256, 512, 8, 16)

        def _split_heads(t, h):
            n, m, c = t.shape
            return t.reshape(n, m, h, c // h).transpose(0, 2, 1, 3).reshape(n * h, m, c // h)
        key = jax.random.key(seed)
        ks = jax.random.split(key, 7)
        f = lambda k, s, sc=1.0: jax.random.normal(k, s, dtype=jnp.float32) * sc
        return {'x': f(ks[0], (N, M, DIM)), 'pos_w': f(ks[1], (DIM, 1, 3), 0.1), 'pos_b': f(ks[2], (DIM,), 0.02), 'qkv_w': f(ks[3], (3 * DIM, DIM), 0.02), 'qkv_b': f(ks[4], (3 * DIM,), 0.02), 'wo_w': f(ks[5], (DIM, DIM), 0.02), 'wo_b': f(ks[6], (DIM,), 0.02)}
    _L1_ffn_all = _L1_ffn_setup()
    _L1_ffn_in = {k: v for k, v in _L1_ffn_all.items() if k in ('pos_w', 'pos_b', 'qkv_w', 'qkv_b', 'wo_w', 'wo_b')}
    del _L1_ffn_all
    return {'x': x, 'src': src, 'dst': dst, 'L0_gnn_wc': _L0_gnn_in['wc'], 'L0_gnn_wn': _L0_gnn_in['wn'], 'L0_gnn_bias': _L0_gnn_in['bias'], 'L0_ffn_ln_g': _L0_ffn_in['ln_g'], 'L0_ffn_ln_b': _L0_ffn_in['ln_b'], 'L0_ffn_Wq': _L0_ffn_in['Wq'], 'L0_ffn_Wk': _L0_ffn_in['Wk'], 'L0_ffn_Wv': _L0_ffn_in['Wv'], 'L0_ffn_Wo': _L0_ffn_in['Wo'], 'L0_ffn_qn_g': _L0_ffn_in['qn_g'], 'L0_ffn_kn_g': _L0_ffn_in['kn_g'], 'L0_ffn_gate_W': _L0_ffn_in['gate_W'], 'L0_ffn_gate_b': _L0_ffn_in['gate_b'], 'L0_ffn_W1': _L0_ffn_in['W1'], 'L0_ffn_b1': _L0_ffn_in['b1'], 'L0_ffn_W2': _L0_ffn_in['W2'], 'L0_ffn_b2': _L0_ffn_in['b2'], 'L1_gnn_W_self': _L1_gnn_in['W_self'], 'L1_gnn_W_neigh': _L1_gnn_in['W_neigh'], 'L1_gnn_bias': _L1_gnn_in['bias'], 'L1_gnn_gamma': _L1_gnn_in['gamma'], 'L1_gnn_beta': _L1_gnn_in['beta'], 'L1_ffn_pos_w': _L1_ffn_in['pos_w'], 'L1_ffn_pos_b': _L1_ffn_in['pos_b'], 'L1_ffn_qkv_w': _L1_ffn_in['qkv_w'], 'L1_ffn_qkv_b': _L1_ffn_in['qkv_b'], 'L1_ffn_wo_w': _L1_ffn_in['wo_w'], 'L1_ffn_wo_b': _L1_ffn_in['wo_b']}

def reference(x, src, dst, L0_gnn_wc, L0_gnn_wn, L0_gnn_bias, L0_ffn_ln_g, L0_ffn_ln_b, L0_ffn_Wq, L0_ffn_Wk, L0_ffn_Wv, L0_ffn_Wo, L0_ffn_qn_g, L0_ffn_kn_g, L0_ffn_gate_W, L0_ffn_gate_b, L0_ffn_W1, L0_ffn_b1, L0_ffn_W2, L0_ffn_b2, L1_gnn_W_self, L1_gnn_W_neigh, L1_gnn_bias, L1_gnn_gamma, L1_gnn_beta, L1_ffn_pos_w, L1_ffn_pos_b, L1_ffn_qkv_w, L1_ffn_qkv_b, L1_ffn_wo_w, L1_ffn_wo_b):
    import jax
    import jax.numpy as jnp

    def _L0_gnn_ref(x, wc, wn, bias, edge_index):
        import jax, jax.numpy as jnp
        import numpy as np
        N = 6250
        IN_CH = 512
        OUT_CH = 512
        DEG = 32
        E = N * DEG
        alpha = x @ wc
        beta = x @ wn
        src, dst = (edge_index[0], edge_index[1])
        sums = jax.ops.segment_sum(beta[dst], src, num_segments=x.shape[0])
        counts = jax.ops.segment_sum(jnp.ones_like(src, dtype=beta.dtype), src, num_segments=x.shape[0])
        gamma = sums / counts[:, None]
        return alpha + gamma + bias

    def _L0_ffn_ref(x, ln_g, ln_b, Wq, Wk, Wv, Wo, qn_g, kn_g, gate_W, gate_b, W1, b1, W2, b2):
        import jax, jax.numpy as jnp
        import numpy as np
        B, N, DIM = (1, 256, 512)
        DH, H = (64, 8)
        E, FF = (8, 256)

        def _layernorm(x, g, b, eps=1e-05):
            mu = jnp.mean(x, axis=-1, keepdims=True)
            var = jnp.mean(jnp.square(x - mu), axis=-1, keepdims=True)
            return (x - mu) * jax.lax.rsqrt(var + eps) * g + b

        def _l2norm(x, eps=1e-12):
            return x / jnp.sqrt(jnp.sum(jnp.square(x), axis=-1, keepdims=True) + eps)
        b, n, d = x.shape
        dh = qn_g.shape[0]
        h = d // dh
        hx = _layernorm(x, ln_g, ln_b)
        q = (hx @ Wq).reshape(b, n, h, dh).transpose(0, 2, 1, 3)
        k = (hx @ Wk).reshape(b, n, h, dh).transpose(0, 2, 1, 3)
        v = (hx @ Wv).reshape(b, n, h, dh).transpose(0, 2, 1, 3)
        scale = jnp.sqrt(jnp.float32(dh))
        q = _l2norm(q) * scale * qn_g
        k = _l2norm(k) * scale * kn_g
        scores = jnp.einsum('bhqd,bhkd->bhqk', q, k) * dh ** (-0.5)
        causal = jnp.tril(jnp.ones((n, n), bool))
        scores = jnp.where(causal, scores, jnp.finfo(scores.dtype).min)
        attn = jax.nn.softmax(scores, axis=-1)
        o = jnp.einsum('bhqk,bhkd->bhqd', attn, v)
        y = o.transpose(0, 2, 1, 3).reshape(b, n, d) @ Wo
        gate = jax.nn.softmax(y @ gate_W + gate_b, axis=-1)
        hid = jax.nn.gelu(jnp.einsum('bnd,edf->bnef', y, W1) + b1)
        eo = jnp.einsum('bnef,efd->bned', hid, W2) + b2
        out = jnp.einsum('bned,bne->bnd', eo, gate)
        return out

    def _L1_gnn_ref(x, edge_src, edge_dst, deg, W_self, W_neigh, bias, gamma, beta):
        import jax, jax.numpy as jnp
        import numpy as np
        N_NODES = 1250
        N_EDGES = 20000
        IN_DIM = 512
        OUT_DIM = 512
        LN_EPS = 1e-05
        n = x.shape[0]
        h_self = jnp.einsum('nd,od->no', x, W_self)
        neigh_sum = jax.ops.segment_sum(x[edge_src], edge_dst, num_segments=n)
        neigh_mean = neigh_sum / jnp.maximum(deg, 1.0)[:, None]
        h_neigh = jnp.einsum('nd,od->no', neigh_mean, W_neigh)
        h = h_self + h_neigh + bias
        mu = jnp.mean(h, axis=-1, keepdims=True)
        var = jnp.mean(jnp.square(h - mu), axis=-1, keepdims=True)
        h = (h - mu) * jax.lax.rsqrt(var + LN_EPS)
        return h * gamma + beta

    def _L1_ffn_ref(x, pos_w, pos_b, qkv_w, qkv_b, wo_w, wo_b):
        import jax, jax.numpy as jnp
        import numpy as np
        from jax import lax
        N, M, DIM, HEADS, TOPK = (4, 256, 512, 8, 16)

        def _split_heads(t, h):
            n, m, c = t.shape
            return t.reshape(n, m, h, c // h).transpose(0, 2, 1, 3).reshape(n * h, m, c // h)
        n, m, c = x.shape
        h = HEADS
        scale = c ** (-0.5)
        pos = lax.conv_general_dilated(x.transpose(0, 2, 1), pos_w, window_strides=(1,), padding=[(1, 1)], feature_group_count=c, dimension_numbers=('NCH', 'OIH', 'NCH'))
        x = x + (pos + pos_b[None, :, None]).transpose(0, 2, 1)
        qkv = x @ qkv_w.T + qkv_b
        q, k, v = jnp.split(qkv, [c, 2 * c], axis=-1)
        q = _split_heads(q, h)
        k = _split_heads(k, h)
        v = _split_heads(v, h)
        qd = lax.stop_gradient(q)
        kd = lax.stop_gradient(k)
        logits = jnp.einsum('bmd,bpd->bmp', qd * scale, kd)
        _, idx = lax.top_k(logits, TOPK)
        gather = jax.vmap(lambda t, i: t[i])
        k_sel = gather(k, idx)
        v_sel = gather(v, idx)
        attn = jax.nn.softmax(jnp.einsum('bmd,bmkd->bmk', q * scale, k_sel), axis=-1)
        out = jnp.einsum('bmk,bmkd->bmd', attn, v_sel)
        d = c // h
        out = out.reshape(n, h, m, d).transpose(0, 2, 1, 3).reshape(n, m, c)
        return out @ wo_w.T + wo_b
    edge_index = jnp.stack([src, dst])
    deg = jnp.maximum(jax.ops.segment_sum(jnp.ones(dst.shape, jnp.float32), dst, num_segments=1250), 1.0)
    x = x + _L0_gnn_ref(_layernorm(x, axis=-1), L0_gnn_wc, L0_gnn_wn, L0_gnn_bias, edge_index)
    x = x + _L0_ffn_ref(_layernorm(x, axis=-1)[None], L0_ffn_ln_g, L0_ffn_ln_b, L0_ffn_Wq, L0_ffn_Wk, L0_ffn_Wv, L0_ffn_Wo, L0_ffn_qn_g, L0_ffn_kn_g, L0_ffn_gate_W, L0_ffn_gate_b, L0_ffn_W1, L0_ffn_b1, L0_ffn_W2, L0_ffn_b2)[0]
    x = x + _L1_gnn_ref(_layernorm(x, axis=-1), src, dst, deg, L1_gnn_W_self, L1_gnn_W_neigh, L1_gnn_bias, L1_gnn_gamma, L1_gnn_beta)
    x = x + _L1_ffn_ref(_layernorm(x, axis=-1)[None], L1_ffn_pos_w, L1_ffn_pos_b, L1_ffn_qkv_w, L1_ffn_qkv_b, L1_ffn_wo_w, L1_ffn_wo_b)[0]
    return x

_drawn_inputs = setup_inputs


def setup_inputs(seed=0):
    import zlib

    import numpy as np

    out = dict(_drawn_inputs(seed))
    spreads = {'L0_ffn_ln_g': (1.0, 0.6),
     'L0_ffn_ln_b': (0.0, 0.8),
     'L0_ffn_qn_g': (1.0, 0.6),
     'L0_ffn_kn_g': (1.0, 0.6),
     'L0_ffn_gate_b': (0.0, 0.8),
     'L0_ffn_b1': (0.0, 2.0),
     'L0_ffn_b2': (0.0, 0.8),
     'L1_gnn_bias': (0.0, 2.0),
     'L1_gnn_gamma': (1.0, 0.6),
     'L1_gnn_beta': (0.0, 2.0)}
    factors = {'L0_ffn_Wq': 8.0,
     'L0_ffn_Wk': 8.0,
     'L0_ffn_Wv': 8.0,
     'L0_ffn_Wo': 8.0,
     'L0_ffn_gate_W': 8.0,
     'L0_ffn_W1': 8.0,
     'L0_ffn_W2': 7.537,
     'L1_ffn_pos_w': 21.616,
     'L1_ffn_pos_b': 64.0,
     'L1_ffn_qkv_b': 44.872,
     'L1_ffn_wo_b': 200.0,
     'L1_gnn_W_self': 5.296,
     'L1_gnn_W_neigh': 7.913,
     'L1_ffn_qkv_w': 8.0,
     'L1_ffn_wo_w': 8.0}
    for name, (base, spread) in spreads.items():
        noise = np.random.default_rng([zlib.crc32(name.encode()), seed]).standard_normal(out[name].shape)
        drawn = base * np.exp(spread * noise) if base else spread * noise
        out[name] = jnp.asarray(drawn.astype(out[name].dtype))
    for name, factor in factors.items():
        out[name] = (out[name] * factor).astype(out[name].dtype)
    return out
```

```python
from contextlib import ExitStack

import concourse.bass as bass
from concourse import mybir

F32 = mybir.dt.float32
F16 = mybir.dt.float16
I32 = mybir.dt.int32
ALU = mybir.AluOpType
ACT = mybir.ActivationFunctionType
AX_X = mybir.AxisListType.X

P = 128
N = 1250
NT = (N + P - 1) // P
NP = NT * P
TAIL = N - (NT - 1) * P
D = 512
KD = D // P
H = 8
DH = D // H
HP = H // 2
NE = 41250
ET = (NE + P - 1) // P
EG = (ET + P - 1) // P
SPAN = 36
FAR = 4096
EX = 8
FF = 256
FB = EX * FF // P
EPS = 1e-5
L2_EPS = 1e-12
MASKED = -1e30
TAKEN = -3e38
CH = 320
NCH = NP // CH
BANK = 512


def pieces(n, most=BANK):
    return [(a, min(most, n - a)) for a in range(0, n, most)]


class Stage:

    def __init__(self, nc, m, ctx, name):
        m.stages += 1
        self.nc, self.ctx, self.name = nc, ctx, f"{name}{m.stages}"

    def signals(self, names):
        return [self.ctx.enter_context(self.nc.semaphore(f"{self.name}_{n}")) for n in names.split()]

    def sb(self, name, shape, dt=F32):
        return self.ctx.enter_context(self.nc.sbuf_tensor(f"{self.name}_{name}", shape, dt))

    def psum(self, name, shape):
        return self.ctx.enter_context(self.nc.psum_tensor(f"{self.name}_{name}", shape, F32))


def load_consts(nc, m, io):
    with ExitStack() as ctx:
        s = Stage(nc, m, ctx, "ld")
        (s_zeroed, s_nodes, s_made, s_small) = s.signals(
            "zeroed nodes made small")
        ruler_i = s.sb("ruler_i", [P, NP], I32)
        block = ctx.enter_context(nc.Block())

        @block.sync
        def _(sp):
            x = io["x"]
            sp.wait_ge(s_zeroed, 1)
            sp.dma_start(m.X[0:TAIL, NT - 1, :], x[(NT - 1) * P:N, :]).then_inc(s_nodes, 16)
            for a in (0, 3, 6):
                sp.dma_start(m.X[:, a:a + 3, :], x[a * P:(a + 3) * P, :].rearrange("(t p) d -> p t d", p=P)
                             ).then_inc(s_nodes, 16)
            sp.wait_ge(s_nodes, 64)

        @block.scalar
        def _(act):
            for vec, name in ((m.bias0, "L0_gnn_bias"), (m.bias1, "L1_gnn_bias"), (m.gamma1, "L1_gnn_gamma"),
                              (m.beta1, "L1_gnn_beta"), (m.wo_b, "L1_ffn_wo_b")):
                act.dma_start(vec[:, :], io[name].rearrange("(a d) -> a d", a=1).broadcast_to([P, D])
                              ).then_inc(s_small, 16)
            act.dma_start(m.v_b[:, :], io["L1_ffn_qkv_b"][2 * D:3 * D].rearrange("(a d) -> a d", a=1)
                          .broadcast_to([P, D])).then_inc(s_small, 16)
            act.wait_ge(s_small, 96)

        @block.gpsimd
        def _(pool):
            pool.memset(m.identf[:, :], 0.0).then_inc(s_made, 1)
            pool.memset(m.causal[:, :], 0.0).then_inc(s_made, 1)
            pool.memset(m.padded[:, :], 0.0).then_inc(s_made, 1)
            pool.memset(m.eps[:, 0:1], EPS).then_inc(s_made, 1)
            pool.memset(m.eps[:, 1:2], L2_EPS).then_inc(s_made, 1)
            pool.memset(m.ones[:, :], 1.0).then_inc(s_made, 1)
            pool.memset(m.sel[:, :, :], 0.0).then_inc(s_made, 1)
            pool.iota(ruler_i[:, :], [[1, NP]], base=0, channel_multiplier=0).then_inc(s_made, 1)
            pool.wait_ge(s_made, 8)
            pool.affine_select(out=m.identf[:, :], in_=m.identf[:, :], compare_op=ALU.not_equal, fill=1.0,
                               base=0, pattern=[[-1, P]], channel_multiplier=1).then_inc(s_made, 1)
            pool.affine_select(out=m.causal[:, :], in_=m.causal[:, :], compare_op=ALU.is_ge, fill=MASKED,
                               base=0, pattern=[[-1, P]], channel_multiplier=1).then_inc(s_made, 1)
            pool.affine_select(out=m.padded[:, NT - 1:NT], in_=m.padded[:, NT - 1:NT], compare_op=ALU.is_ge,
                               fill=1.0, base=TAIL - 1, pattern=[[0, 1]], channel_multiplier=-1
                               ).then_inc(s_made, 1)
            pool.affine_select(out=m.sel[:, :, :], in_=m.sel[:, :, :], compare_op=ALU.not_equal, fill=1.0,
                               base=0, pattern=[[-1, EX], [0, P]], channel_multiplier=1).then_inc(s_made, 1)

        @block.vector
        def _(dve):
            dve.memset(m.X[:, NT - 1, :], 0.0).then_inc(s_zeroed, 1)
            dve.wait_ge(s_made, 12)
            dve.tensor_copy(m.ruler[:, :], ruler_i[:, :])
            dve.tensor_copy(m.ident16[:, :], m.identf[:, :])
            for t in range(NT):
                if t == 0:
                    dve.wait_ge(s_nodes, 64)
                dve.bn_stats(m.stats[:, t, :], m.X[:, t, :])


def norm_scales(nc, m, twice=False):
    with ExitStack() as ctx:
        s = Stage(nc, m, ctx, "ns")
        (s_step, s_root) = s.signals(
            "step root")
        tmp = s.sb("tmp", [P, 3, NT])
        block = ctx.enter_context(nc.Block())

        @block.scalar
        def _(act):
            act.wait_ge(s_step, NT)
            act.activation(tmp[:, 0, :], m.mv[:, :, 1], ACT.Sqrt, bias=m.eps[:, 0:1]).then_inc(s_root, 1)
            if twice:
                act.wait_ge(s_step, NT + 3)
                act.activation(tmp[:, 2, :], tmp[:, 1, :], ACT.Sqrt, bias=m.eps[:, 0:1]).then_inc(s_root, 1)

        @block.vector
        def _(dve):
            for t in range(NT):
                dve.bn_aggr(m.mv[:, t, :], m.stats[:, t, :]).then_inc(s_step, 1)
            dve.wait_ge(s_root, 1)
            dve.reciprocal(m.scale[:, :], tmp[:, 0, :]).then_inc(s_step, 1)
            n = NT + 1
            dve.wait_ge(s_step, n)
            if twice:
                dve.tensor_tensor(tmp[:, 1, :], m.mv[:, :, 1], m.scale[:, :], ALU.mult).then_inc(s_step, 1)
                dve.wait_ge(s_step, n + 1)
                dve.tensor_tensor(tmp[:, 1, :], tmp[:, 1, :], m.scale[:, :], ALU.mult).then_inc(s_step, 1)
                dve.wait_ge(s_root, 2)
                dve.reciprocal(tmp[:, 2, :], tmp[:, 2, :]).then_inc(s_step, 1)
                dve.wait_ge(s_step, n + 3)
                dve.tensor_tensor(m.scale[:, :], m.scale[:, :], tmp[:, 2, :], ALU.mult).then_inc(s_step, 1)
                n += 4
                dve.wait_ge(s_step, n)
            dve.scalar_tensor_tensor(out=m.shift[:, :], in0=m.mv[:, :, 0], scalar=-1.0, in1=m.scale[:, :],
                                     op0=ALU.mult, op1=ALU.mult)


def count_edges(nc, m, io):
    with ExitStack() as ctx:
        s = Stage(nc, m, ctx, "ce")
        (s_blank, s_edges, s_cast, s_turned, s_cols, s_onehot, s_used, s_closed, s_drained, s_flipped,
         s_kept, s_tiles, s_plan, s_lined, s_row, s_far) = s.signals(
            "blank edges cast turned cols onehot used closed drained flipped kept tiles plan lined row far")
        raw = s.sb("raw", [P, 2, EG, P], I32)
        rawf = s.sb("rawf", [P, 2, EG, P])
        ends = s.sb("ends", [P, 2, EG * P])
        hot_d = s.sb("hot_d", [P, 2, P], F16)
        hot_s = s.sb("hot_s", [P, 2, N], F16)
        none = s.sb("none", [P, P], F16)
        tile_i = s.sb("tile_i", [P, EG], I32)
        tile_f = s.sb("tile_f", [P, EG])
        bounds = s.sb("bounds", [P, 2, EG])
        some = s.sb("some", [P, EG, P])
        plan = s.sb("plan", [P, 2, NT, EG])
        lined = s.sb("lined", [2 * NT, 1])
        row = s.sb("row", [1, 2 * NT + 1])
        row_i = s.sb("row_i", [1, 2 * NT + 1], I32)
        ps_e = s.psum("ps_e", [P, 2, BANK])
        ps_a = s.psum("ps_a", [P, 3 * BANK])
        ps_p = s.psum("ps_p", [2 * NT, BANK])
        ps_r = s.psum("ps_r", [1, BANK])
        block = ctx.enter_context(nc.Block())
        full = NE // P
        rest = NE - full * P
        last_g, last_p = full // P, full % P
        pairs = (ET + 1) // 2

        @block.sync
        def _(sp):
            sp.wait_ge(s_blank, 1)
            for n, name in enumerate(("src", "dst")):
                e = io[name]
                for g in range(EG):
                    rows = min(P, full - g * P)
                    sp.dma_start(raw[0:rows, n, g, :], e[g * P * P:(g * P + rows) * P].rearrange(
                        "(t p) -> t p", p=P)).then_inc(s_edges, 16)
                sp.dma_start(raw[last_p:last_p + 1, n, last_g, 0:rest], e[full * P:NE].rearrange(
                    "(a p) -> a p", a=1)).then_inc(s_edges, 16)

        @block.gpsimd
        def _(pool):
            pool.iota(tile_i[:, :], [[P, EG]], base=0, channel_multiplier=1).then_inc(s_tiles, 1)

        @block.vector
        def _(dve):
            dve.memset(raw[:, :, :, :], -1).then_inc(s_blank, 1)
            dve.memset(none[:, :], 0.0).then_inc(s_blank, 1)
            dve.wait_ge(s_tiles, 1)
            dve.tensor_copy(tile_f[:, :], tile_i[:, :]).then_inc(s_plan, 1)
            dve.wait_ge(s_edges, 16 * 2 * (EG + 1))
            dve.tensor_copy(rawf[:, :, :, :], raw[:, :, :, :]).then_inc(s_cast, 1)
            dve.wait_ge(s_cast, 1)
            dve.tensor_reduce(bounds[:, 0, :], rawf[:, 1, :, :], AX_X, ALU.max).then_inc(s_plan, 1)
            dve.tensor_scalar(some[:, :, :], rawf[:, 1, :, :], 0.0, float(FAR), ALU.is_lt, ALU.mult
                              ).then_inc(s_plan, 1)
            dve.wait_ge(s_plan, 3)
            dve.tensor_tensor(some[:, :, :], some[:, :, :], rawf[:, 1, :, :], ALU.add).then_inc(s_plan, 1)
            dve.wait_ge(s_plan, 4)
            dve.tensor_reduce(bounds[:, 1, :], some[:, :, :], AX_X, ALU.min).then_inc(s_plan, 1)
            dve.wait_ge(s_plan, 5)
            for j in range(NT):
                dve.tensor_scalar(plan[:, 0, j, :], bounds[:, 0, :], float(j * P), float(FAR), ALU.is_lt, ALU.mult
                                  ).then_inc(s_far, 1)
                dve.tensor_scalar(plan[:, 1, j, :], bounds[:, 1, :], float((j + 1) * P), float(FAR), ALU.is_ge,
                                  ALU.mult).then_inc(s_far, 1)
            dve.wait_ge(s_far, 2 * NT)
            tiles = tile_f[:, :].unsqueeze(1).broadcast_to([P, NT, EG])
            dve.tensor_tensor(plan[:, 0, :, :], plan[:, 0, :, :], tiles, ALU.add).then_inc(s_plan, 1)
            dve.tensor_tensor(plan[:, 1, :, :], plan[:, 1, :, :], tiles, ALU.subtract).then_inc(s_plan, 1)
            dve.wait_ge(s_turned, 1)
            dve.tensor_copy(ends[:, :, :], ps_e[:, :, 0:EG * P]).then_inc(s_cols, 1)
            dve.wait_ge(s_lined, 1)
            dve.tensor_reduce(lined[:, :], ps_p[:, 0:EG * P], AX_X, ALU.min).then_inc(s_row, 1)
            dve.wait_ge(s_lined, 2)
            dve.tensor_copy(row[:, 0:2 * NT], ps_r[:, 0:2 * NT]).then_inc(s_row, 1)
            dve.wait_ge(s_row, 2)
            dve.tensor_tensor(row[:, NT:2 * NT], row[:, NT:2 * NT], row[:, 0:NT], ALU.add).then_inc(s_row, 1)
            dve.wait_ge(s_row, 3)
            dve.tensor_reduce(row[:, 2 * NT:2 * NT + 1], row[:, NT:2 * NT], AX_X, ALU.min).then_inc(s_row, 1)
            dve.wait_ge(s_row, 4)
            dve.tensor_scalar(row[:, 2 * NT:2 * NT + 1], row[:, 2 * NT:2 * NT + 1], float(1 - SPAN), None,
                              ALU.is_lt).then_inc(s_row, 1)
            dve.tensor_scalar(row[:, 0:NT], row[:, 0:NT], float(EG * P - SPAN), None, ALU.min).then_inc(s_row, 1)
            dve.wait_ge(s_row, 6)
            dve.tensor_copy(row_i[:, :], row[:, :]).then_inc(s_row, 1)
            dve.wait_ge(s_cols, 1)
            dve.wait_ge(s_row, 7)
            for opened in (s_onehot,):
                dve.sem_inc(opened, 1)

            def one_hots(count, all_tiles):
                with dve.Fori(0, NT) as j:
                    first = 0 if all_tiles else dve.value_load(row_i[0:1, bass.ds(j, 1)], min_val=0,
                                                               max_val=EG * P - SPAN)
                    with dve.Fori(0, count) as i:
                        for u in range(2):
                            e = 2 * i + u + first
                            dve.wait_ge(s_used, j * (2 * count) + 2 * i + u + 1)
                            dve.tensor_scalar(hot_d[:, u, :], m.ruler[:, bass.ts(j, P)], ends[:, 1, bass.ds(e, 1)],
                                              None, ALU.is_equal)
                            dve.tensor_scalar(hot_s[:, u, :], m.ruler[:, 0:N], ends[:, 0, bass.ds(e, 1)], None,
                                              ALU.is_equal).then_inc(s_onehot, 1)

            scattered = dve.value_load(row_i[0:1, 2 * NT:2 * NT + 1], min_val=0, max_val=1)
            with dve.If(scattered):
                one_hots(pairs, True)
            with dve.Else():
                one_hots(SPAN // 2, False)

        @block.tensor
        def _(pe):
            pe.sem_inc(s_used, 1)
            pe.wait_ge(s_cast, 1)
            for n in range(2):
                for g in range(EG):
                    mm = pe.transpose(ps_e[:, n, g * P:(g + 1) * P], rawf[:, n, g, :], m.identf[:, :])
            mm.then_inc(s_turned, 1)
            pe.wait_ge(s_plan, 7)
            for g in range(EG):
                mm = pe.transpose(ps_p[:, g * P:(g + 1) * P], plan[:, :, :, g].rearrange("p a j -> p (a j)"),
                                  m.identf[:, :])
            mm.then_inc(s_lined, 1)
            pe.wait_ge(s_row, 1)
            pe.transpose(ps_r[:, 0:2 * NT], lined[:, :], m.identf[0:2 * NT, 0:2 * NT]).then_inc(s_lined, 1)
            pe.wait_ge(s_cols, 1)
            pe.wait_ge(s_blank, 2)
            pe.wait_ge(s_row, 7)
            pe.matmul(ps_a[:, 0:P], none[:, :], none[:, :], start=True, stop=True).then_inc(s_used, 1)

            def products(count):
                with pe.Fori(0, NT) as j:
                    pe.wait_ge(s_drained, j + 1)
                    for a, w in pieces(NP):
                        pe.matmul(ps_a[:, a:a + w], none[:, :], m.ruler[:, a:a + w], start=True, stop=False)
                    with pe.Fori(0, count) as i:
                        for u in range(2):
                            pe.wait_ge(s_onehot, j * (2 * count) + 2 * i + u + 2)
                            for a, w in pieces(N):
                                mm = pe.matmul(ps_a[:, a:a + w], hot_d[:, u, :], hot_s[:, u, a:a + w],
                                               start=False, stop=False)
                            mm.then_inc(s_used, 1)
                    for a, w in pieces(NP):
                        mm = pe.matmul(ps_a[:, a:a + w], none[:, :], m.ruler[:, a:a + w], start=False, stop=True)
                    mm.then_inc(s_closed, 1)

            scattered = pe.value_load(row_i[0:1, 2 * NT:2 * NT + 1], min_val=0, max_val=1)
            with pe.If(scattered):
                products(pairs)
            with pe.Else():
                products(SPAN // 2)
            pe.wait_ge(s_drained, NT + 1)
            with pe.Fori(0, NT) as j:
                pe.wait_ge(s_kept, j + 1)
                for b in range(NT):
                    mm = pe.matmul(ps_a[:, b * P:(b + 1) * P], m.A[:, b, bass.ts(j, P)], m.ident16[:, :],
                                   start=True, stop=True)
                mm.then_inc(s_flipped, 1)

        @block.scalar
        def _(act):
            for opened in (s_drained, s_kept):
                act.sem_inc(opened, 1)
            with act.Fori(0, NT) as j:
                act.wait_ge(s_closed, j + 1)
                act.activation(m.A[:, bass.ds(j, 1), :], ps_a[:, 0:NP], ACT.Copy,
                               accum_out=m.deg_d[:, bass.ds(j, 1)]).then_inc(s_drained, 1)
            with act.Fori(0, NT) as j:
                act.wait_ge(s_flipped, j + 1)
                act.activation(m.AT[:, bass.ds(j, 1), :], ps_a[:, 0:NP], ACT.Copy,
                               accum_out=m.deg_s[:, bass.ds(j, 1)]).then_inc(s_kept, 1)


def node_rows(nc, m, xn, hi, lo):
    with ExitStack() as ctx:
        s = Stage(nc, m, ctx, "nr")
        (s_rows, s_high) = s.signals(
            "rows high")
        block = ctx.enter_context(nc.Block())

        @block.scalar
        def _(act):
            for t in range(NT):
                act.activation(xn[:, t, :], m.X[:, t, :], ACT.Identity, bias=m.shift[:, t:t + 1],
                               scale=m.scale[:, t:t + 1]).then_inc(s_rows, 1)

        @block.vector
        def _(dve):
            for t in range(NT):
                dve.wait_ge(s_rows, t + 1)
                dve.tensor_copy(hi[:, t, :], xn[:, t, :]).then_inc(s_high, 1)

        @block.gpsimd
        def _(pool):
            for t in range(NT):
                pool.wait_ge(s_high, t + 1)
                pool.tensor_tensor(lo[:, t, :], xn[:, t, :], hi[:, t, :], ALU.subtract)


def aggregate(nc, m, hi, lo, adj, agg):
    with ExitStack() as ctx:
        s = Stage(nc, m, ctx, "ag")
        (s_summed, s_kept_v, s_kept_a) = s.signals(
            "summed kept_v kept_a")
        ps = s.psum("ps", [P, KD, BANK])
        block = ctx.enter_context(nc.Block())

        @block.tensor
        def _(pe):
            with pe.Fori(0, NCH) as c:
                for f in range(KD):
                    pe.wait_ge(s_kept_a if f % 2 else s_kept_v, 2 * c + 1)
                    for t in range(NT):
                        for part in (hi, lo):
                            mm = pe.matmul(ps[:, f, 0:CH], part[:, t, f * P:(f + 1) * P],
                                           adj[:, t, bass.ts(c, CH)],
                                           start=(t == 0 and part is hi), stop=(t == NT - 1 and part is lo))
                    mm.then_inc(s_summed, 1)

        @block.vector
        def _(dve):
            for opened in (s_kept_v,):
                dve.sem_inc(opened, 1)
            with dve.Fori(0, NCH) as c:
                for f in (0, 2):
                    dve.wait_ge(s_summed, KD * c + f + 1)
                    dve.tensor_copy(agg[:, f, bass.ts(c, CH)], ps[:, f, 0:CH]).then_inc(s_kept_v, 1)

        @block.scalar
        def _(act):
            for opened in (s_kept_a,):
                act.sem_inc(opened, 1)
            with act.Fori(0, NCH) as c:
                for f in (1, 3):
                    act.wait_ge(s_summed, KD * c + f + 1)
                    act.copy(agg[:, f, bass.ts(c, CH)], ps[:, f, 0:CH]).then_inc(s_kept_a, 1)


def graph_rows(nc, m, xn, agg, w_own, w_near, deg, bias, affine=None):
    with ExitStack() as ctx:
        s = Stage(nc, m, ctx, "gr")
        (s_inv, s_rows_in, s_near_in, s_cols, s_own_done, s_near_done, s_step, s_free_ps, s_free_t,
         s_root, s_passed) = s.signals(
            "inv rows_in near_in cols own_done near_done step free_ps free_t root passed")
        xs = s.sb("xs", [P, 2, D])
        near = s.sb("near", [P, 2, KD, P])
        xt = s.sb("xt", [P, 2, KD, P])
        hsum = s.sb("hsum", [P, 2, D])
        st = s.sb("st", [P, 2, 6])
        mv = s.sb("mvh", [P, 2, 2])
        sc = s.sb("sc", [P, 2, 3])
        inv = s.sb("inv", [P, NT])
        ps_t = s.psum("ps_t", [P, 2, KD, P])
        ps_n = s.psum("ps_n", [P, 2, BANK])
        ps_o = s.psum("ps_o", [P, 2, BANK])
        block = ctx.enter_context(nc.Block())

        @block.gpsimd
        def _(pool):
            with pool.Fori(0, NT // 2) as i:
                for u in range(2):
                    pool.wait_ge(s_free_t, 2 * i + 1)
                    pool.tensor_copy(xs[:, u, :], xn[:, bass.ds(2 * i + u, 1), :]).then_inc(s_rows_in, 1)

        @block.scalar
        def _(act):
            with act.Fori(0, NT // 2) as i:
                for u in range(2):
                    t = 2 * i + u
                    act.wait_ge(s_near_done, 2 * i + 1)
                    act.copy(near[:, u, :, :], agg[:, :, bass.ts(t, P)]).then_inc(s_near_in, 1)
                    if affine:
                        act.wait_ge(s_step, 9 * t + 4)
                        act.activation(sc[:, u, 0:1], mv[:, u, 1:2], ACT.Sqrt, bias=m.eps[:, 0:1]
                                       ).then_inc(s_root, 1)

        @block.tensor
        def _(pe):
            for opened in (s_free_t, s_near_done, s_own_done):
                pe.sem_inc(opened, 1)
            with pe.Fori(0, NT // 2) as i:
                for u in range(2):
                    t = 2 * i + u
                    pe.wait_ge(s_rows_in, t + 1)
                    pe.wait_ge(s_cols, 2 * i + 1)
                    for k in range(KD):
                        mm = pe.transpose(ps_t[:, u, k, :], xs[:, u, k * P:(k + 1) * P], m.identf[:, :])
                    mm.then_inc(s_free_t, 1)
                    pe.wait_ge(s_near_in, t + 1)
                    pe.wait_ge(s_free_ps, 2 * i + 1)
                    for k in range(KD):
                        mm = pe.matmul(ps_n[:, u, :], near[:, u, k, :], w_near[:, k, :],
                                       start=(k == 0), stop=(k == KD - 1))
                    mm.then_inc(s_near_done, 1)
                    pe.wait_ge(s_cols, t + 2)
                    for k in range(KD):
                        mm = pe.matmul(ps_o[:, u, :], xt[:, u, k, :], w_own[:, k, :],
                                       start=(k == 0), stop=(k == KD - 1))
                    mm.then_inc(s_own_done, 1)

        @block.vector
        def _(dve):
            for opened in (s_cols, s_free_ps):
                dve.sem_inc(opened, 1)
            dve.tensor_tensor(inv[:, :], deg[:, :], m.padded[:, :], ALU.add).then_inc(s_inv, 1)
            n = 1
            if affine:
                dve.wait_ge(s_inv, 1)
                dve.tensor_scalar(inv[:, :], inv[:, :], 1.0, None, ALU.max).then_inc(s_inv, 1)
                n = 2
            dve.wait_ge(s_inv, n)
            dve.reciprocal(inv[:, :], inv[:, :]).then_inc(s_inv, 1)
            dve.wait_ge(s_inv, n + 1)
            c = 9 if affine else 3
            with dve.Fori(0, NT // 2) as i:
                for u in range(2):
                    t = 2 * i + u
                    hs, x_t = hsum[:, u, :], m.X[:, bass.ds(t, 1), :]
                    dve.wait_ge(s_free_t, t + 2)
                    dve.wait_ge(s_own_done, 2 * i + 1)
                    dve.tensor_copy(xt[:, u, :, :], ps_t[:, u, :, :]).then_inc(s_cols, 1)
                    dve.wait_ge(s_near_done, t + 2)
                    dve.scalar_tensor_tensor(out=hs, in0=ps_n[:, u, :], scalar=inv[:, bass.ds(t, 1)],
                                             in1=bias[:, :], op0=ALU.mult, op1=ALU.add).then_inc(s_step, 1)
                    dve.wait_ge(s_own_done, t + 2)
                    dve.wait_ge(s_step, c * t + 1)
                    dve.tensor_tensor(hs, hs, ps_o[:, u, :], ALU.add).then_inc(s_step, 1)
                    dve.wait_ge(s_step, c * t + 2)
                    if affine:
                        dve.bn_stats(st[:, u, :], hs).then_inc(s_step, 1)
                        dve.wait_ge(s_step, c * t + 3)
                        dve.sem_inc(s_passed, 1)
                        dve.bn_aggr(mv[:, u, :], st[:, u, :]).then_inc(s_step, 1)
                        dve.wait_ge(s_root, t + 1)
                        dve.reciprocal(sc[:, u, 1:2], sc[:, u, 0:1]).then_inc(s_step, 1)
                        dve.wait_ge(s_step, c * t + 5)
                        dve.tensor_scalar(hs, hs, mv[:, u, 0:1], sc[:, u, 1:2],
                                          ALU.subtract, ALU.mult).then_inc(s_step, 1)
                        dve.wait_ge(s_step, c * t + 6)
                        dve.tensor_tensor(hs, hs, affine[0][:, :], ALU.mult).then_inc(s_step, 1)
                        dve.wait_ge(s_step, c * t + 7)
                        dve.tensor_tensor(hs, hs, affine[1][:, :], ALU.add).then_inc(s_step, 1)
                        dve.wait_ge(s_step, c * t + 8)
                    dve.tensor_tensor(x_t, x_t, hsum[:, u:u + 1, :], ALU.add).then_inc(s_step, 1)
                    dve.wait_ge(s_step, c * t + c)
                    dve.bn_stats(m.stats[:, bass.ds(t, 1), :], x_t).then_inc(s_free_ps, 1)


def turn_weights(nc, m, raws, outs):
    with ExitStack() as ctx:
        s = Stage(nc, m, ctx, "tw")
        (s_turned, s_kept) = s.signals(
            "turned kept")
        ps = s.psum("ps", [P, 2, KD, P])
        block = ctx.enter_context(nc.Block())
        work = [(raw, out, b) for raw, out in zip(raws, outs) for b in range(raw.shape[1])]

        @block.tensor
        def _(pe):
            for n, (raw, out, b) in enumerate(work):
                if n >= 2:
                    pe.wait_ge(s_kept, n - 1)
                for k in range(KD):
                    mm = pe.transpose(ps[:, n % 2, k, :], raw[:, b, k * P:(k + 1) * P], m.identf[:, :])
                mm.then_inc(s_turned, 1)

        @block.vector
        def _(dve):
            for n, (raw, out, b) in enumerate(work):
                dve.wait_ge(s_turned, n + 1)
                dve.tensor_copy(out[:, :, b * P:(b + 1) * P], ps[:, n % 2, :, :]).then_inc(s_kept, 1)


def causal_qkv(nc, m, io, QO, KT, V):
    with ExitStack() as ctx:
        s = Stage(nc, m, ctx, "cq")
        (s_wts, s_rows, s_turned, s_cols, s_q_ps, s_k_ps, s_v_ps, s_v_kept, s_sq, s_summed, s_root,
         s_step, s_qk_turned, s_q_kept, s_k_kept, s_gained) = s.signals(
            "wts rows turned cols q_ps k_ps v_ps v_kept sq summed root step qk_turned "
            "q_kept k_kept gained")
        wq = s.sb("wq", [P, KD, D])
        wk = s.sb("wk", [P, KD, D])
        wv = s.sb("wv", [P, KD, D])
        gains = s.sb("gains", [P, 2 * KD + 2])
        hn = s.sb("hn", [P, 2, D])
        ht = s.sb("ht", [P, 2, KD, P])
        sq = s.sb("sq", [P, 2, D])
        ss = s.sb("ss", [P, 3, 2, H])
        qn = s.sb("qn", [P, 2, D])
        ps_t = s.psum("ps_t", [P, 2, KD, P])
        ps_q = s.psum("ps_q", [P, 2, BANK])
        ps_v = s.psum("ps_v", [P, BANK])
        ps_r = s.psum("ps_r", [P, 2, KD, P])
        block = ctx.enter_context(nc.Block())

        @block.sync
        def _(sp):
            for w, name in ((wq, "L0_ffn_Wq"), (wk, "L0_ffn_Wk"), (wv, "L0_ffn_Wv")):
                sp.dma_start(w[:, :, :], io[name].rearrange("(k p) n -> p k n", p=P)).then_inc(s_wts, 16)
            for c, name in ((0, "L0_ffn_ln_g"), (KD, "L0_ffn_ln_b")):
                sp.dma_start(gains[:, c:c + KD], io[name].rearrange("(k p) -> p k", p=P)).then_inc(s_wts, 16)
            for c, name in ((2 * KD, "L0_ffn_qn_g"), (2 * KD + 1, "L0_ffn_kn_g")):
                for half in range(2):
                    sp.dma_start(gains[half * DH:(half + 1) * DH, c:c + 1],
                                 io[name].rearrange("(p a) -> p a", a=1)).then_inc(s_wts, 16)
            sp.wait_ge(s_wts, 16 * 9)

        @block.scalar
        def _(act):
            for opened in (s_v_kept, s_q_kept, s_k_kept, s_root):
                act.sem_inc(opened, 1)
            act.wait_ge(s_wts, 16 * 9)
            act.wait_ge(s_gained, 1)
            with act.Fori(0, NT // 2) as i:
                for u in range(2):
                    t = 2 * i + u
                    act.wait_ge(s_turned, 2 * i + 1)
                    act.activation(hn[:, u, :], m.X[:, bass.ds(t, 1), :], ACT.Identity,
                                   bias=m.shift[:, bass.ds(t, 1)], scale=m.scale[:, bass.ds(t, 1)]
                                   ).then_inc(s_rows, 1)
                    for n, done in enumerate((s_q_ps, s_k_ps)):
                        act.wait_ge(done, t + 1)
                        act.wait_ge(s_summed, 2 * t + 1)
                        act.activation(sq[:, n, :], ps_q[:, n, :], ACT.Square).then_inc(s_sq, 1)
                    act.wait_ge(s_v_ps, t + 2)
                    act.copy(V[:, bass.ds(t, 1), :], ps_v[:, :]).then_inc(s_v_kept, 1)
                    act.wait_ge(s_summed, 2 * t + 3)
                    act.activation(ss[:, 1, :, :], ss[:, 0, :, :], ACT.Sqrt, bias=m.eps[:, 1:2]).then_inc(s_root, 1)
                    act.wait_ge(s_qk_turned, 2 * t + 2)
                    act.activation(QO[:, :, bass.ts(t, P)], ps_r[:, 0, :, :], ACT.Copy,
                                   scale=gains[:, 2 * KD:2 * KD + 1]).then_inc(s_q_kept, 1)
                    act.wait_ge(s_qk_turned, 2 * t + 3)
                    act.activation(KT[:, :, bass.ts(t, P)], ps_r[:, 1, :, :], ACT.Copy,
                                   scale=gains[:, 2 * KD + 1:2 * KD + 2]).then_inc(s_k_kept, 1)

        @block.vector
        def _(dve):
            for opened in (s_summed, s_cols, s_step):
                dve.sem_inc(opened, 1)
            dve.wait_ge(s_wts, 16 * 9)
            dve.tensor_scalar(gains[:, 2 * KD + 1:2 * KD + 2], gains[:, 2 * KD + 1:2 * KD + 2], float(DH) ** 0.5,
                              None, ALU.mult).then_inc(s_gained, 1)
            with dve.Fori(0, NT // 2) as i:
                for u in range(2):
                    t = 2 * i + u
                    dve.wait_ge(s_turned, t + 2)
                    dve.wait_ge(s_v_ps, 2 * i + 1)
                    for k in range(KD):
                        ins = dve.tensor_scalar(ht[:, u, k, :], ps_t[:, u, k, :], gains[:, k:k + 1],
                                                gains[:, KD + k:KD + k + 1], ALU.mult, ALU.add)
                    ins.then_inc(s_cols, 1)
                    for n in range(2):
                        dve.wait_ge(s_sq, 2 * t + n + 1)
                        if n == 0:
                            dve.wait_ge(s_root, t + 1)
                        dve.tensor_reduce(ss[:, 0, n, :], sq[:, n, :].rearrange("p (h d) -> p h d", h=H),
                                          AX_X, ALU.add).then_inc(s_summed, 1)
                    dve.wait_ge(s_root, t + 2)
                    dve.reciprocal(ss[:, 2, :, :], ss[:, 1, :, :]).then_inc(s_step, 1)
                    dve.wait_ge(s_step, 3 * t + 2)
                    for n in range(2):
                        dve.wait_ge(s_qk_turned, 2 * t + n + 1)
                        dve.tensor_tensor(qn[:, n, :].rearrange("p (h d) -> p h d", h=H),
                                          ps_q[:, n, :].rearrange("p (h d) -> p h d", h=H),
                                          ss[:, 2, n, :].unsqueeze(2).broadcast_to([P, H, DH]), ALU.mult
                                          ).then_inc(s_step, 1)

        @block.tensor
        def _(pe):
            for opened in (s_turned, s_qk_turned, s_v_ps):
                pe.sem_inc(opened, 1)
            pe.wait_ge(s_wts, 16 * 9)
            with pe.Fori(0, NT // 2) as i:
                for u in range(2):
                    t = 2 * i + u
                    pe.wait_ge(s_rows, t + 1)
                    pe.wait_ge(s_cols, 2 * i + 1)
                    for k in range(KD):
                        mm = pe.transpose(ps_t[:, u, k, :], hn[:, u, k * P:(k + 1) * P], m.identf[:, :])
                    mm.then_inc(s_turned, 1)
                    pe.wait_ge(s_cols, t + 2)
                    pe.wait_ge(s_step, 3 * t + 1)
                    for w, ps, done in ((wq, ps_q[:, 0, :], s_q_ps), (wk, ps_q[:, 1, :], s_k_ps),
                                        (wv, ps_v[:, :], s_v_ps)):
                        if w is wv:
                            pe.wait_ge(s_v_kept, t + 1)
                        for k in range(KD):
                            mm = pe.matmul(ps, ht[:, u, k, :], w[:, k, :], start=(k == 0), stop=(k == KD - 1))
                        mm.then_inc(done, 1)
                    for n, kept in enumerate((s_q_kept, s_k_kept)):
                        pe.wait_ge(s_step, 3 * t + 2 + n + 1)
                        pe.wait_ge(kept, t + 1)
                        for k in range(KD):
                            mm = pe.transpose(ps_r[:, n, k, :], qn[:, n, k * P:(k + 1) * P], m.identf[:, :])
                        mm.then_inc(s_qk_turned, 1)


def attention(nc, m, QO, KT, V, top, prefetch=None):
    steps = [(half, t) for half in range(2) for t in range(NT)]
    SN = len(steps)
    width = [NP if top else (t + 1) * P for _, t in steps]
    groups = [pieces(w) for w in width]
    before = [sum(len(g) for g in groups[:n]) for n in range(SN + 1)]
    GN = before[SN]
    s_bufs, t_bufs = (1, 4) if top else (2, 1)
    with ExitStack() as ctx:
        s = Stage(nc, m, ctx, "at")
        (s_clear, s_staged, s_scored, s_s_free, s_masked, s_maxed, s_topped, s_expd, s_probs,
         s_turned, s_pt_kept, s_o_done, s_o_kept, s_step, s_passed) = s.signals(
            "clear staged scored s_free masked maxed topped expd probs turned pt_kept "
            "o_done o_kept step passed")
        qs = s.sb("qs", [P, NP])
        ks = s.sb("ks", [P, NP])
        vs = s.sb("vs", [P, NT, P])
        pr = s.sb("pr", [P, 2, NP])
        pt = s.sb("pt", [P, 2, NP])
        negm = s.sb("negm", [P, 2])
        ssum = s.sb("ssum", [P, 2])
        rsum = s.sb("rsum", [P, 2])
        if top:
            sc = s.sb("sc", [P, 2, N])
            work = s.sb("work", [P, N])
            m8 = s.sb("m8", [P, 2, 8])
        ps_s = [s.psum(f"ps_s{b}", [P, 3 * BANK]) for b in range(s_bufs)]
        ps_t = s.psum("ps_t", [P, t_bufs, BANK])
        ps_o = s.psum("ps_o", [P, BANK])
        block = ctx.enter_context(nc.Block())

        if prefetch:
            @block.sync
            def _(sp):
                prefetch(sp)

        @block.gpsimd
        def _(pool):
            with pool.Fori(0, HP) as i:
                pool.wait_ge(s_o_done, SN * i + 1)
                pool.tensor_copy(qs[:, :], QO[:, bass.ds(i, 1), :]).then_inc(s_staged, 1)

        @block.tensor
        def _(pe):
            for opened in (s_o_done, s_turned):
                pe.sem_inc(opened, 1)
            with pe.Fori(0, HP) as i:
                pe.wait_ge(s_staged, 3 * i + 3)

                def scores(n):
                    half, t = steps[n]
                    r = slice(half * DH, (half + 1) * DH)
                    pe.wait_ge(s_s_free, SN * i + max(n + 1 - s_bufs, 0) + 1)
                    for a, w in pieces(width[n]):
                        mm = pe.matmul(ps_s[n % s_bufs][:, a:a + w], qs[r, t * P:(t + 1) * P], ks[r, a:a + w],
                                       start=True, stop=True)
                    mm.then_inc(s_scored, 1)

                def turn(n, g):
                    c = before[n] + g
                    if g == 0:
                        pe.wait_ge(s_probs if top else s_s_free, SN * i + n + 2)
                    pe.wait_ge(s_pt_kept, GN * i + max(c + 1 - t_bufs, 0) + 1)
                    a, w = groups[n][g]
                    for b in range(w // P):
                        mm = pe.transpose(ps_t[:, c % t_bufs, b * P:(b + 1) * P],
                                          pr[:, n % 2, a + b * P:a + (b + 1) * P], m.identf[:, :])
                    mm.then_inc(s_turned, 1)

                def weigh(n, g):
                    half, t = steps[n]
                    pe.wait_ge(s_pt_kept, GN * i + before[n] + g + 2)
                    if g == 0:
                        pe.wait_ge(s_o_kept, SN * i + n + 1)
                    a, w = groups[n][g]
                    for k in range(a // P, (a + w) // P):
                        mm = pe.matmul(ps_o[:, 0:DH], pt[:, n % 2, k * P:(k + 1) * P],
                                       vs[:, k, half * DH:(half + 1) * DH],
                                       start=(k == 0), stop=(k == width[n] // P - 1))
                    if g == len(groups[n]) - 1:
                        mm.then_inc(s_o_done, 1)

                scores(0)
                for n in range(SN):
                    if top and n + 1 < SN:
                        scores(n + 1)
                    turn(n, 0)
                    if not top and n + 1 < SN:
                        scores(n + 1)
                    for g in range(1, len(groups[n])):
                        turn(n, g)
                        weigh(n, g - 1)
                    weigh(n, len(groups[n]) - 1)

        @block.scalar
        def _(act):
            for opened in (s_s_free, s_pt_kept):
                act.sem_inc(opened, 1)
            with act.Fori(0, HP) as i:
                act.wait_ge(s_o_done, SN * i + 1)
                act.copy(vs[:, :, :], V[:, :, bass.ts(i, P)]).then_inc(s_staged, 1)

                def keep(n):
                    for g, (a, w) in enumerate(groups[n]):
                        c = before[n] + g
                        act.wait_ge(s_turned, GN * i + c + 2)
                        if g == 0:
                            act.wait_ge(s_o_done, SN * i + max(n - 1, 0) + 1)
                        act.copy(pt[:, n % 2, a:a + w], ps_t[:, c % t_bufs, 0:w]).then_inc(s_pt_kept, 1)

                for n in range(SN + 1):
                    if n < SN and top:
                        act.wait_ge(s_scored, SN * i + n + 1)
                        act.wait_ge(s_topped, SN * i + max(n - 1, 0) + 1)
                        act.copy(sc[:, n % 2, :], ps_s[0][:, 0:N]).then_inc(s_s_free, 1)
                    if n < SN:
                        act.wait_ge(s_maxed, SN * i + n + 1)
                        act.wait_ge(s_turned, GN * i + before[max(n - 1, 0)] + 1)
                        if top:
                            act.activation(pr[:, n % 2, 0:N], sc[:, n % 2, :], ACT.Exp, bias=negm[:, n % 2:n % 2 + 1]
                                           ).then_inc(s_expd, 1)
                        else:
                            act.wait_ge(s_o_kept, SN * i + max(n - 1, 0) + 1)
                            act.activation(pr[:, n % 2, 0:width[n]], ps_s[n % 2][:, 0:width[n]], ACT.Exp,
                                           bias=negm[:, n % 2:n % 2 + 1],
                                           accum_out=ssum[:, n % 2:n % 2 + 1]).then_inc(s_s_free, 1)
                    if top and n >= 1:
                        keep(n - 1)
                    if not top and n < SN:
                        keep(n)

        @block.vector
        def _(dve):
            for opened in (s_o_kept, s_topped, s_probs):
                dve.sem_inc(opened, 1)
            if top:
                dve.memset(pr[:, :, N:NP], 0.0).then_inc(s_clear, 1)
                dve.wait_ge(s_clear, 1)

            with dve.Fori(0, HP) as i:
                dve.wait_ge(s_o_done, SN * i + 1)
                dve.tensor_copy(ks[:, :], KT[:, bass.ds(i, 1), 0:NP]).then_inc(s_staged, 1)

                def divide(n):
                    half, t = steps[n]
                    dve.wait_ge(s_o_done, SN * i + n + 2)
                    dve.reciprocal(rsum[:, n % 2:n % 2 + 1], ssum[:, n % 2:n % 2 + 1]).then_inc(s_step, 1)
                    dve.wait_ge(s_step, SN * i + n + 1)
                    dve.tensor_scalar(QO[:, bass.ds(i, 1), t * P + half * DH:t * P + (half + 1) * DH],
                                      ps_o[:, 0:DH], rsum[:, n % 2:n % 2 + 1], None, ALU.mult).then_inc(s_o_kept, 1)

                for n in range(SN):
                    half, t = steps[n]
                    g = SN * i + n
                    nm = negm[:, n % 2:n % 2 + 1]
                    if not top:
                        dve.wait_ge(s_scored, g + 1)
                        own = ps_s[n % 2][:, t * P:(t + 1) * P]
                        dve.tensor_tensor(own, own, m.causal[:, :], ALU.add).then_inc(s_masked, 1)
                        dve.wait_ge(s_masked, g + 1)
                        dve.wait_ge(s_s_free, SN * i + max(n - 1, 0) + 1)
                        dve.tensor_reduce(nm, ps_s[n % 2][:, 0:width[n]], AX_X, ALU.max, negate=True
                                          ).then_inc(s_maxed, 1)
                    else:
                        dve.wait_ge(s_s_free, g + 2)
                        dve.sem_inc(s_passed, 1)
                        dve.max(m8[:, 0, :], sc[:, n % 2, :]).then_inc(s_masked, 1)
                        dve.wait_ge(s_masked, 3 * g + 1)
                        dve.tensor_scalar(nm, m8[:, 0, 0:1], -1.0, None, ALU.mult).then_inc(s_maxed, 1)
                        dve.wait_ge(s_probs, g + 1)
                        dve.sem_inc(s_passed, 1)
                        dve.match_replace(work[:, :], m8[:, 0, :], sc[:, n % 2, :], TAKEN).then_inc(s_masked, 1)
                        dve.wait_ge(s_masked, 3 * g + 2)
                        dve.sem_inc(s_passed, 1)
                        dve.max(m8[:, 1, :], work[:, :]).then_inc(s_masked, 1)
                        dve.wait_ge(s_masked, 3 * g + 3)
                        dve.sem_inc(s_passed, 1)
                        dve.match_replace(work[:, :], m8[:, 1, :], work[:, :], TAKEN).then_inc(s_topped, 1)
                        dve.wait_ge(s_topped, g + 2)
                        dve.wait_ge(s_expd, g + 1)
                        p = pr[:, n % 2, 0:N]
                        dve.scalar_tensor_tensor(out=p, in0=work[:, :], scalar=TAKEN, in1=p, op0=ALU.is_equal,
                                                 op1=ALU.mult, accum_out=ssum[:, n % 2:n % 2 + 1]
                                                 ).then_inc(s_probs, 1)
                    if n >= 1:
                        divide(n - 1)
                divide(SN - 1)


def experts(nc, m, io, QO, w1, w2, wts, weights2):
    with ExitStack() as ctx:
        s = Stage(nc, m, ctx, "ex")
        (s_small, s_w2, s_rows, s_turned, s_cols, s_y_ps, s_y_kept, s_logits, s_expd, s_step, s_gate,
         s_gate_t, s_gate_row, s_spread, s_hid, s_gelu, s_mixed, s_out, s_added) = s.signals(
            "small w2 rows turned cols y_ps y_kept logits expd step gate gate_t gate_row "
            "spread hid gelu mixed out added")
        wo = s.sb("wo", [P, KD, D])
        gw = s.sb("gw", [P, KD, EX])
        gb = s.sb("gb", [1, EX])
        b1 = s.sb("b1", [P, FB])
        b2 = s.sb("b2", [EX, D])
        os_ = s.sb("os_", [P, 2, KD, P])
        ot = s.sb("ot", [P, 2, KD, P])
        yt = s.sb("yt", [P, 2, KD, P])
        hid = s.sb("hid", [P, FB, P])
        g = s.sb("g", [P, 4, EX])
        gt = s.sb("gt", [EX, P])
        ps_t = s.psum("ps_t", [P, KD, P])
        ps_y = s.psum("ps_y", [P, KD, P])
        ps_g = s.psum("ps_g", [P, BANK])
        ps_b = s.psum("ps_b", [P, EX, P])
        ps_h = s.psum("ps_h", [P, 2, 4, P])
        ps_x = s.psum("ps_x", [P, BANK])
        block = ctx.enter_context(nc.Block())
        QB = FB // 4

        @block.sync
        def _(sp):
            sp.dma_start(wo[:, :, :], io["L0_ffn_Wo"].rearrange("(k p) n -> p k n", p=P)).then_inc(s_small, 16)
            sp.dma_start(gw[:, :, :], io["L0_ffn_gate_W"].rearrange("(k p) e -> p k e", p=P)).then_inc(s_small, 16)
            sp.dma_start(gb[:, :], io["L0_ffn_gate_b"].rearrange("(a e) -> a e", a=1)).then_inc(s_small, 16)
            sp.dma_start(b1[:, :], io["L0_ffn_b1"].rearrange("e (b p) -> p (e b)", p=P)).then_inc(s_small, 16)
            sp.dma_start(b2[:, :], io["L0_ffn_b2"]).then_inc(s_small, 16)
            weights2(sp, s_w2)
            sp.wait_ge(s_small, 80)

        @block.gpsimd
        def _(pool):
            with pool.Fori(0, NT // 2) as i:
                for u in range(2):
                    t = 2 * i + u
                    pool.wait_ge(s_turned, 2 * i + 1)
                    pool.tensor_copy(os_[:, u, :, :], QO[:, :, bass.ts(t, P)]).then_inc(s_rows, 1)

        @block.tensor
        def _(pe):
            for opened in (s_turned, s_out, s_y_ps, s_gate_t):
                pe.sem_inc(opened, 1)
            pe.wait_ge(s_small, 80)
            pe.wait_ge(wts[0], wts[1])
            pe.wait_ge(s_w2, 32)
            with pe.Fori(0, NT // 2) as i:
                for u in range(2):
                    t = 2 * i + u
                    pe.wait_ge(s_rows, t + 1)
                    pe.wait_ge(s_cols, t + 1)
                    for k in range(KD):
                        mm = pe.transpose(ps_t[:, k, :], os_[:, u, k, :], m.identf[:, :])
                    mm.then_inc(s_turned, 1)
                    pe.wait_ge(s_cols, t + 2)
                    pe.wait_ge(s_y_kept, t + 1)
                    for f in range(KD):
                        for k in range(KD):
                            mm = pe.matmul(ps_y[:, f, :], wo[:, k, f * P:(f + 1) * P], ot[:, u, k, :],
                                           start=(k == 0), stop=(k == KD - 1))
                    mm.then_inc(s_y_ps, 1)
                    pe.wait_ge(s_y_kept, t + 2)
                    pe.wait_ge(s_gate_row, t + 1)
                    for k in range(KD):
                        pe.matmul(ps_g[:, 0:EX], yt[:, u, k, :], gw[:, k, :], start=(k == 0), stop=False)
                    pe.matmul(ps_g[:, 0:EX], m.ones[0:1, :], gb[:, :], start=False, stop=True).then_inc(s_logits, 1)
                    for q in range(QB):
                        pe.wait_ge(s_gelu, 4 * (QB * t) + 4 * max(q - 1, 0) + 1)
                        for b in range(4):
                            f = 4 * q + b
                            for k in range(KD):
                                mm = pe.matmul(ps_h[:, q % 2, b, :], w1[:, k, f * P:(f + 1) * P], yt[:, u, k, :],
                                               start=(k == 0), stop=(k == KD - 1))
                        mm.then_inc(s_hid, 1)
                    pe.wait_ge(s_gate, t + 1)
                    pe.transpose(ps_g[0:EX, P:2 * P], g[:, 3, :], m.identf[:, :]).then_inc(s_gate_t, 1)
                    pe.wait_ge(s_gate_row, t + 2)
                    for e in range(EX):
                        mm = pe.matmul(ps_b[:, e, :], m.sel[:, e, :], gt[:, :], start=True, stop=True)
                    mm.then_inc(s_spread, 1)
                    pe.wait_ge(s_added, t + 1)
                    pe.matmul(ps_x[:, :], gt[:, :], b2[:, :], start=True, stop=False)
                    for q in range(QB):
                        pe.wait_ge(s_mixed, QB * t + q + 1)
                        for b in range(4):
                            f = 4 * q + b
                            mm = pe.matmul(ps_x[:, :], hid[:, f, :], w2[:, f, :], start=False, stop=(f == FB - 1))
                    mm.then_inc(s_out, 1)

        @block.scalar
        def _(act):
            for opened in (s_y_kept, s_gelu):
                act.sem_inc(opened, 1)
            act.wait_ge(s_small, 80)
            with act.Fori(0, NT // 2) as i:
                for u in range(2):
                    t = 2 * i + u
                    act.wait_ge(s_y_ps, t + 2)
                    act.copy(yt[:, u, :, :], ps_y[:, :, :]).then_inc(s_y_kept, 1)
                    act.wait_ge(s_step, 3 * t + 1)
                    act.activation(g[:, 0, :], ps_g[:, 0:EX], ACT.Exp, bias=g[:, 1, 0:1],
                                   accum_out=g[:, 1, 1:2]).then_inc(s_expd, 1)
                    act.wait_ge(s_out, t + 1)
                    for q in range(QB):
                        act.wait_ge(s_hid, QB * t + q + 1)
                        for b in range(4):
                            f = 4 * q + b
                            act.activation(hid[:, f, :], ps_h[:, q % 2, b, :], ACT.Gelu_apprx_tanh,
                                           bias=b1[:, f:f + 1]).then_inc(s_gelu, 1)

        @block.vector
        def _(dve):
            for opened in (s_cols, s_gate_row, s_added):
                dve.sem_inc(opened, 1)
            with dve.Fori(0, NT // 2) as i:
                for u in range(2):
                    t = 2 * i + u
                    dve.wait_ge(s_turned, t + 2)
                    dve.wait_ge(s_y_ps, 2 * i + 1)
                    dve.tensor_copy(ot[:, u, :, :], ps_t[:, :, :]).then_inc(s_cols, 1)
                    dve.wait_ge(s_logits, t + 1)
                    dve.tensor_reduce(g[:, 1, 0:1], ps_g[:, 0:EX], AX_X, ALU.max, negate=True).then_inc(s_step, 1)
                    dve.wait_ge(s_expd, t + 1)
                    dve.reciprocal(g[:, 1, 2:3], g[:, 1, 1:2]).then_inc(s_step, 1)
                    dve.wait_ge(s_step, 3 * t + 2)
                    dve.wait_ge(s_gate_t, t + 1)
                    dve.tensor_scalar(g[:, 3, :], g[:, 0, :], g[:, 1, 2:3], None, ALU.mult).then_inc(s_gate, 1)
                    dve.wait_ge(s_gate_t, t + 2)
                    dve.wait_ge(s_out, t + 1)
                    dve.tensor_copy(gt[:, :], ps_g[0:EX, P:2 * P]).then_inc(s_gate_row, 1)
                    dve.wait_ge(s_spread, t + 1)
                    for q in range(QB):
                        dve.wait_ge(s_gelu, 4 * (QB * t) + 4 * q + 4 + 1)
                        for e in range(2):
                            h2 = hid[:, 4 * q + 2 * e:4 * q + 2 * e + 2, :]
                            ins = dve.tensor_tensor(h2, h2, ps_b[:, 2 * q + e, :].unsqueeze(1).broadcast_to([P, 2, P]),
                                                    ALU.mult)
                        ins.then_inc(s_mixed, 1)
                    dve.wait_ge(s_out, t + 2)
                    x_t = m.X[:, bass.ds(t, 1), :]
                    dve.tensor_tensor(x_t, x_t, ps_x[:, :].unsqueeze(1), ALU.add).then_inc(s_added, 1)
                    dve.wait_ge(s_added, t + 2)
                    dve.bn_stats(m.stats[:, bass.ds(t, 1), :], x_t).then_inc(s_step, 1)


def conv_cols(nc, m, io, ct):
    with ExitStack() as ctx:
        s = Stage(nc, m, ctx, "cv")
        (s_small, s_rows, s_turned, s_cols, s_edge, s_mid, s_step) = s.signals(
            "small rows turned cols edge mid step")
        z = s.sb("z", [P, KD, NP + 2])
        zn = s.sb("zn", [P, 2, D])
        taps = s.sb("taps", [P, KD, 4])
        ps_t = s.psum("ps_t", [P, 2, KD, P])
        block = ctx.enter_context(nc.Block())

        @block.sync
        def _(sp):
            sp.dma_start(taps[:, :, 0:3], io["L1_ffn_pos_w"].rearrange("(k p) a c -> p k (a c)", p=P)
                         ).then_inc(s_small, 16)
            sp.dma_start(taps[:, :, 3:4], io["L1_ffn_pos_b"].rearrange("(k p a) -> p k a", p=P, a=1)
                         ).then_inc(s_small, 16)
            sp.wait_ge(s_small, 32)

        @block.tensor
        def _(pe):
            for opened in (s_turned,):
                pe.sem_inc(opened, 1)
            with pe.Fori(0, NT // 2) as i:
                for u in range(2):
                    pe.wait_ge(s_rows, 2 * i + u + 1)
                    pe.wait_ge(s_cols, 2 * i + 1)
                    for k in range(KD):
                        mm = pe.transpose(ps_t[:, u, k, :], zn[:, u, k * P:(k + 1) * P], m.identf[:, :])
                    mm.then_inc(s_turned, 1)

        @block.scalar
        def _(act):
            with act.Fori(0, NT // 2) as i:
                for u in range(2):
                    t = 2 * i + u
                    act.wait_ge(s_turned, 2 * i + 1)
                    act.activation(zn[:, u, :], m.X[:, bass.ds(t, 1), :], ACT.Identity,
                                   bias=m.shift[:, bass.ds(t, 1)], scale=m.scale[:, bass.ds(t, 1)]
                                   ).then_inc(s_rows, 1)
            act.wait_ge(s_small, 32)
            act.wait_ge(s_edge, 2)
            for k in range(KD):
                act.activation(ct[:, k, :], z[:, k, 1:NP + 1], ACT.Identity, scale=taps[:, k, 1:2],
                               bias=taps[:, k, 3:4]).then_inc(s_mid, 1)

        @block.vector
        def _(dve):
            for opened in (s_cols,):
                dve.sem_inc(opened, 1)
            with dve.Fori(0, NT // 2) as i:
                for u in range(2):
                    t = 2 * i + u
                    dve.wait_ge(s_turned, t + 2)
                    dve.tensor_copy(z[:, :, bass.ds(t * P + 1, P)], ps_t[:, u, :, :]).then_inc(s_cols, 1)
            dve.wait_ge(s_cols, NT + 1)
            dve.memset(z[:, :, 0:1], 0.0).then_inc(s_edge, 1)
            dve.memset(z[:, :, N + 1:NP + 2], 0.0).then_inc(s_edge, 1)
            dve.wait_ge(s_edge, 2)
            dve.wait_ge(s_small, 32)
            for k in range(KD):
                dve.wait_ge(s_mid, k + 1)
                for n, tap in enumerate((0, 2)):
                    dve.scalar_tensor_tensor(out=ct[:, k, :], in0=z[:, k, tap:tap + NP], scalar=taps[:, k, tap:tap + 1],
                                             in1=ct[:, k, :], op0=ALU.mult, op1=ALU.add).then_inc(s_step, 1)
                    dve.wait_ge(s_step, 3 * k + n + 1)
                dve.tensor_tensor(ct[:, k, :], ct[:, k, :], z[:, k, 1:NP + 1], ALU.add).then_inc(s_step, 1)


def top_qkv(nc, m, io, ct, wt, QO, KT, V):
    with ExitStack() as ctx:
        s = Stage(nc, m, ctx, "tq")
        (s_small, s_projected, s_kept, s_cut, s_v_ps, s_v_kept) = s.signals(
            "small projected kept cut v_ps v_kept")
        qb = s.sb("qb", [P, 2 * KD])
        cs = s.sb("cs", [P, 2, KD, P])
        ps = s.psum("ps", [P, 4, BANK])
        ps_v = s.psum("ps_v", [P, 2, BANK])
        block = ctx.enter_context(nc.Block())
        scale = float(D) ** -0.5

        @block.sync
        def _(sp):
            sp.dma_start(qb[:, :], io["L1_ffn_qkv_b"][0:2 * D].rearrange("(k p) -> p k", p=P)).then_inc(s_small, 16)
            sp.wait_ge(s_small, 16)

        @block.tensor
        def _(pe):
            for opened in (s_v_ps,):
                pe.sem_inc(opened, 1)
            with pe.Fori(0, NCH) as c:
                for f in range(2 * KD):
                    pe.wait_ge(s_kept, 2 * KD * c + max(f - 3, 0) + 1)
                    for k in range(KD):
                        mm = pe.matmul(ps[:, f % 4, 0:CH], wt[:, k, f * P:(f + 1) * P], ct[:, k, bass.ts(c, CH)],
                                       start=(k == 0), stop=(k == KD - 1))
                    mm.then_inc(s_projected, 1)
            with pe.Fori(0, NT // 2) as i:
                for u in range(2):
                    t = 2 * i + u
                    pe.wait_ge(s_cut, t + 1)
                    pe.wait_ge(s_v_kept, 2 * i + 1)
                    for k in range(KD):
                        mm = pe.matmul(ps_v[:, u, :], cs[:, u, k, :], wt[:, k, 2 * D:3 * D],
                                       start=(k == 0), stop=(k == KD - 1))
                    mm.then_inc(s_v_ps, 1)

        @block.scalar
        def _(act):
            with act.Fori(0, NT // 2) as i:
                for u in range(2):
                    t = 2 * i + u
                    act.wait_ge(s_v_ps, 2 * i + 1)
                    act.copy(cs[:, u, :, :], ct[:, :, bass.ts(t, P)]).then_inc(s_cut, 1)

        @block.vector
        def _(dve):
            for opened in (s_kept, s_v_kept):
                dve.sem_inc(opened, 1)
            dve.wait_ge(s_small, 16)
            with dve.Fori(0, NCH) as c:
                for f in range(2 * KD):
                    dve.wait_ge(s_projected, 2 * KD * c + f + 1)
                    out = (QO if f < KD else KT)[:, f % KD, bass.ts(c, CH)]
                    dve.tensor_scalar(out, ps[:, f % 4, 0:CH], qb[:, f:f + 1], scale if f < KD else 1.0,
                                      ALU.add, ALU.mult).then_inc(s_kept, 1)
            with dve.Fori(0, NT // 2) as i:
                for u in range(2):
                    t = 2 * i + u
                    dve.wait_ge(s_v_ps, t + 2)
                    dve.tensor_tensor(V[:, bass.ds(t, 1), :], ps_v[:, u:u + 1, :], m.v_b[:, :].unsqueeze(1), ALU.add
                                      ).then_inc(s_v_kept, 1)


def project_out(nc, m, QO, wo, out):
    with ExitStack() as ctx:
        s = Stage(nc, m, ctx, "po")
        (s_rows, s_turned, s_cols, s_ps, s_step, s_final, s_stored) = s.signals(
            "rows turned cols ps step final stored")
        os_ = s.sb("os_", [P, 2, KD, P])
        ot = s.sb("ot", [P, 2, KD, P])
        ps_t = s.psum("ps_t", [P, 2, KD, P])
        ps_x = s.psum("ps_x", [P, 2, BANK])
        block = ctx.enter_context(nc.Block())

        @block.gpsimd
        def _(pool):
            with pool.Fori(0, NT // 2) as i:
                for u in range(2):
                    pool.wait_ge(s_turned, 2 * i + 1)
                    pool.tensor_copy(os_[:, u, :, :], QO[:, :, bass.ts(2 * i + u, P)]).then_inc(s_rows, 1)

        @block.tensor
        def _(pe):
            for opened in (s_turned, s_ps):
                pe.sem_inc(opened, 1)
            with pe.Fori(0, NT // 2) as i:
                for u in range(2):
                    t = 2 * i + u
                    pe.wait_ge(s_rows, t + 1)
                    pe.wait_ge(s_cols, 2 * i + 1)
                    for k in range(KD):
                        mm = pe.transpose(ps_t[:, u, k, :], os_[:, u, k, :], m.identf[:, :])
                    mm.then_inc(s_turned, 1)
                    pe.wait_ge(s_cols, t + 2)
                    pe.wait_ge(s_final, 2 * i + 1)
                    for k in range(KD):
                        mm = pe.matmul(ps_x[:, u, :], ot[:, u, k, :], wo[:, k, :], start=(k == 0), stop=(k == KD - 1))
                    mm.then_inc(s_ps, 1)

        @block.vector
        def _(dve):
            for opened in (s_cols, s_final):
                dve.sem_inc(opened, 1)
            with dve.Fori(0, NT // 2) as i:
                for u in range(2):
                    t = 2 * i + u
                    x_t = m.X[:, bass.ds(t, 1), :]
                    dve.wait_ge(s_turned, t + 2)
                    dve.wait_ge(s_ps, 2 * i + 1)
                    dve.tensor_copy(ot[:, u, :, :], ps_t[:, u, :, :]).then_inc(s_cols, 1)
                    dve.tensor_tensor(x_t, x_t, m.wo_b[:, :].unsqueeze(1), ALU.add).then_inc(s_step, 1)
                    dve.wait_ge(s_step, t + 1)
                    dve.wait_ge(s_ps, t + 2)
                    dve.tensor_tensor(x_t, x_t, ps_x[:, u:u + 1, :], ALU.add).then_inc(s_final, 1)

        @block.sync
        def _(sp):
            for t in range(NT):
                rows = P if t < NT - 1 else TAIL
                sp.wait_ge(s_final, t + 2)
                sp.dma_start(out[t * P:t * P + rows, :], m.X[0:rows, t, :]).then_inc(s_stored, 16)
            sp.wait_ge(s_stored, 16 * NT)


def load(nc, name, pairs):
    with ExitStack() as ctx:
        done = ctx.enter_context(nc.semaphore(f"{name}_loaded"))
        block = ctx.enter_context(nc.Block())

        @block.sync
        def _(sp):
            for dst, src in pairs:
                sp.dma_start(dst, src).then_inc(done, 16)
            sp.wait_ge(done, 16 * len(pairs))


def rows_of(w):
    return w.rearrange("(k p) n -> p k n", p=P)


class Memory:

    def __init__(self, nc, ctx):
        def sb(name, shape, dt=F32):
            return ctx.enter_context(nc.sbuf_tensor(name, shape, dt))

        self.stages = 0
        self.X = sb("X", [P, NT, D])
        self.AT = sb("AT", [P, NT, NP], F16)
        self.identf = sb("identf", [P, P])
        self.ident16 = sb("ident16", [P, P], F16)
        self.ruler = sb("ruler", [P, NP], F16)
        self.causal = sb("causal", [P, P])
        self.ones = sb("ones", [P, P])
        self.sel = sb("sel", [EX, EX, P])
        self.padded = sb("padded", [P, NT])
        self.eps = sb("eps", [P, 2])
        self.stats = sb("stats", [P, NT, 6])
        self.mv = sb("mv", [P, NT, 2])
        self.scale = sb("scale", [P, NT])
        self.shift = sb("shift", [P, NT])
        self.deg_s = sb("deg_s", [P, NT])
        self.deg_d = sb("deg_d", [P, NT])
        self.bias0, self.bias1, self.gamma1, self.beta1, self.wo_b, self.v_b = (
            sb(name, [P, D]) for name in ("bias0", "bias1", "gamma1", "beta1", "wo_b", "v_b"))


def build(nc, io, out):
    with ExitStack() as whole, nc.allow_non_contiguous_dma(reason="vectors of a few hundred elements"):
        m = Memory(nc, whole)
        load_consts(nc, m, io)
        with ExitStack() as ctx:
            m.A = ctx.enter_context(nc.sbuf_tensor("A", [P, NT, NP], F16))
            wc = ctx.enter_context(nc.sbuf_tensor("wc", [P, KD, D], F32))
            wn = ctx.enter_context(nc.sbuf_tensor("wn", [P, KD, D], F32))
            count_edges(nc, m, io)
            load(nc, "g0", [(wc[:, :, :], rows_of(io["L0_gnn_wc"])), (wn[:, :, :], rows_of(io["L0_gnn_wn"]))])
            graph_layer(nc, m, m.A, m.deg_s, wc, wn, m.bias0)
        with ExitStack() as ctx:
            QO = ctx.enter_context(nc.sbuf_tensor("QO", [P, KD, NP], F32))
            with ExitStack() as att:
                KT = att.enter_context(nc.sbuf_tensor("KT", [P, KD, NP], F32))
                V = att.enter_context(nc.sbuf_tensor("V", [P, NT, D], F32))
                norm_scales(nc, m, twice=True)
                causal_qkv(nc, m, io, QO, KT, V)
                attention(nc, m, QO, KT, V, top=False)
            w1 = ctx.enter_context(nc.sbuf_tensor("w1", [P, KD, EX * FF], F32))
            w2 = ctx.enter_context(nc.sbuf_tensor("w2", [P, FB, D], F32))
            w1_in = ctx.enter_context(nc.semaphore("w1_in"))

            def load_experts(sp, sem):
                for e in range(EX):
                    sp.dma_start(w1[:, :, e * FF:(e + 1) * FF], rows_of(io["L0_ffn_W1"][e])).then_inc(w1_in, 16)
                w2_rows = io["L0_ffn_W2"].rearrange("e (b p) n -> p (e b) n", p=P)
                for half in range(2):
                    a = half * FB // 2
                    sp.dma_start(w2[:, a:a + FB // 2, :], w2_rows[:, a:a + FB // 2, :]).then_inc(sem, 16)

            experts(nc, m, io, QO, w1, w2, (w1_in, 16 * EX), load_experts)
        with ExitStack() as ctx:
            raw = ctx.enter_context(nc.sbuf_tensor("raw_g", [P, 2, KD, D], F32))
            ws = ctx.enter_context(nc.sbuf_tensor("ws", [P, KD, D], F32))
            wn = ctx.enter_context(nc.sbuf_tensor("wn1", [P, KD, D], F32))
            load(nc, "g1", [(raw[:, 0, :, :], rows_of(io["L1_gnn_W_self"])),
                            (raw[:, 1, :, :], rows_of(io["L1_gnn_W_neigh"]))])
            turn_weights(nc, m, [raw[:, 0, :, :], raw[:, 1, :, :]], [ws, wn])
            graph_layer(nc, m, m.AT, m.deg_d, ws, wn, m.bias1, affine=(m.gamma1, m.beta1))
        with ExitStack() as ctx:
            QO = ctx.enter_context(nc.sbuf_tensor("QO1", [P, KD, NP], F32))
            KT = ctx.enter_context(nc.sbuf_tensor("KT1", [P, KD, NP], F32))
            V = ctx.enter_context(nc.sbuf_tensor("V1", [P, NT, D], F32))
            wo = ctx.enter_context(nc.sbuf_tensor("wo1", [P, KD, D], F32))
            norm_scales(nc, m)
            with ExitStack() as pre:
                wt = pre.enter_context(nc.sbuf_tensor("wt", [P, KD, 3 * D], F32))
                with ExitStack() as r:
                    raw = r.enter_context(nc.sbuf_tensor("raw_q", [P, 4 * KD, D], F32))
                    load(nc, "f1", [(raw[:, 0:3 * KD, :], rows_of(io["L1_ffn_qkv_w"])),
                                    (raw[:, 3 * KD:4 * KD, :], rows_of(io["L1_ffn_wo_w"]))])
                    turn_weights(nc, m, [raw[:, 0:3 * KD, :], raw[:, 3 * KD:4 * KD, :]], [wt, wo])
                ct = pre.enter_context(nc.sbuf_tensor("ct", [P, KD, NP], F32))
                conv_cols(nc, m, io, ct)
                top_qkv(nc, m, io, ct, wt, QO, KT, V)
            attention(nc, m, QO, KT, V, top=True)
            project_out(nc, m, QO, wo, out)


def graph_layer(nc, m, adj, deg, w_own, w_near, bias, affine=None):
    with ExitStack() as ctx:
        s = Stage(nc, m, ctx, "gl")
        xn = s.sb("xn", [P, NT, D])
        agg = s.sb("agg", [P, KD, NP])
        norm_scales(nc, m)
        with ExitStack() as parts:
            p = Stage(nc, m, parts, "gp")
            hi = p.sb("hi", [P, NT, D], F16)
            lo = p.sb("lo", [P, NT, D], F16)
            node_rows(nc, m, xn, hi, lo)
            aggregate(nc, m, hi, lo, adj, agg)
        graph_rows(nc, m, xn, agg, w_own, w_near, deg, bias, affine)


_INS = ["x", "src", "dst", "L0_gnn_wc", "L0_gnn_wn", "L0_gnn_bias", "L0_ffn_ln_g", "L0_ffn_ln_b", "L0_ffn_Wq",
        "L0_ffn_Wk", "L0_ffn_Wv", "L0_ffn_Wo", "L0_ffn_qn_g", "L0_ffn_kn_g", "L0_ffn_gate_W", "L0_ffn_gate_b",
        "L0_ffn_W1", "L0_ffn_b1", "L0_ffn_W2", "L0_ffn_b2", "L1_gnn_W_self", "L1_gnn_W_neigh", "L1_gnn_bias",
        "L1_gnn_gamma", "L1_gnn_beta", "L1_ffn_pos_w", "L1_ffn_pos_b", "L1_ffn_qkv_w", "L1_ffn_qkv_b",
        "L1_ffn_wo_w", "L1_ffn_wo_b"]


def kernel(**inputs):
    import numpy as np
    from concourse import bacc
    from concourse.bass_utils import run_bass_kernel_spmd

    nc = bacc.Bacc("TRN2", target_bir_lowering=False, num_devices=1)
    arrays, io = {}, {}
    for name in _INS:
        a = np.ascontiguousarray(inputs[name])
        arrays[f"in_{name}"] = a
        io[name] = nc.dram_tensor(f"in_{name}", a.shape, mybir.dt.from_np(a.dtype), kind="ExternalInput").ap()
    out = nc.dram_tensor("out_x", (N, D), F32, kind="ExternalOutput").ap()
    build(nc, io, out)
    r = run_bass_kernel_spmd(nc, [arrays], core_ids=[0])
    return r.results[0]["out_x"]
```

```python
from contextlib import ExitStack

import concourse.bass as bass
from concourse import mybir

F32 = mybir.dt.float32
F16 = mybir.dt.float16
F32R = mybir.dt.float32r
I32 = mybir.dt.int32
ALU = mybir.AluOpType
ACT = mybir.ActivationFunctionType
AX_X = mybir.AxisListType.X

P = 128
N = 1250
NT = (N + P - 1) // P
NP = NT * P
TAIL = N - (NT - 1) * P
D = 512
KD = D // P
H = 8
DH = D // H
HP = H // 2
NE = 41250
ET = (NE + P - 1) // P
EG = (ET + P - 1) // P
EARLY = 6
HOTS = 4
SPAN = 36
FAR = 4096
EX = 8
FF = 256
FB = EX * FF // P
EPS = 1e-5
L2_EPS = 1e-12
MASKED = -1e30
TAKEN = -3e38
CH = 320
NCH = NP // CH
BANK = 512


def pieces(n, most=BANK):
    return [(a, min(most, n - a)) for a in range(0, n, most)]


class Stage:

    def __init__(self, nc, m, ctx, name):
        m.stages += 1
        self.nc, self.ctx, self.name = nc, ctx, f"{name}{m.stages}"

    def signals(self, names):
        return [self.ctx.enter_context(self.nc.semaphore(f"{self.name}_{n}")) for n in names.split()]

    def sb(self, name, shape, dt=F32):
        return self.ctx.enter_context(self.nc.sbuf_tensor(f"{self.name}_{name}", shape, dt))

    def psum(self, name, shape):
        return self.ctx.enter_context(self.nc.psum_tensor(f"{self.name}_{name}", shape, F32))


def load_consts(nc, m, io):
    with ExitStack() as ctx:
        s = Stage(nc, m, ctx, "ld")
        (s_zeroed, s_nodes, s_made, s_small) = s.signals(
            "zeroed nodes made small")
        ruler_i = s.sb("ruler_i", [P, NP], I32)
        block = ctx.enter_context(nc.Block())

        @block.sync
        def _(sp):
            x = io["x"]
            sp.wait_ge(s_zeroed, 1)
            sp.dma_start(m.X[0:TAIL, NT - 1, :], x[(NT - 1) * P:N, :]).then_inc(s_nodes, 16)
            for a in (0, 3, 6):
                sp.dma_start(m.X[:, a:a + 3, :], x[a * P:(a + 3) * P, :].rearrange("(t p) d -> p t d", p=P)
                             ).then_inc(s_nodes, 16)
            sp.wait_ge(s_nodes, 64)

        @block.scalar
        def _(act):
            for vec, name in ((m.bias0, "L0_gnn_bias"), (m.bias1, "L1_gnn_bias"), (m.gamma1, "L1_gnn_gamma"),
                              (m.beta1, "L1_gnn_beta"), (m.wo_b, "L1_ffn_wo_b")):
                act.dma_start(vec[:, :], io[name].rearrange("(a d) -> a d", a=1).broadcast_to([P, D])
                              ).then_inc(s_small, 16)
            act.dma_start(m.v_b[:, :], io["L1_ffn_qkv_b"][2 * D:3 * D].rearrange("(a d) -> a d", a=1)
                          .broadcast_to([P, D])).then_inc(s_small, 16)
            act.wait_ge(s_small, 96)

        @block.gpsimd
        def _(pool):
            pool.memset(m.identf[:, :], 0.0).then_inc(s_made, 1)
            pool.memset(m.causal[:, :], 0.0).then_inc(s_made, 1)
            pool.memset(m.padded[:, :], 0.0).then_inc(s_made, 1)
            pool.memset(m.eps[:, 0:1], EPS).then_inc(s_made, 1)
            pool.memset(m.eps[:, 1:2], L2_EPS).then_inc(s_made, 1)
            pool.memset(m.ones[:, :], 1.0).then_inc(s_made, 1)
            pool.memset(m.sel[:, :, :], 0.0).then_inc(s_made, 1)
            pool.iota(ruler_i[:, :], [[1, NP]], base=0, channel_multiplier=0).then_inc(s_made, 1)
            pool.wait_ge(s_made, 8)
            pool.affine_select(out=m.identf[:, :], in_=m.identf[:, :], compare_op=ALU.not_equal, fill=1.0,
                               base=0, pattern=[[-1, P]], channel_multiplier=1).then_inc(s_made, 1)
            pool.affine_select(out=m.causal[:, :], in_=m.causal[:, :], compare_op=ALU.is_ge, fill=MASKED,
                               base=0, pattern=[[-1, P]], channel_multiplier=1).then_inc(s_made, 1)
            pool.affine_select(out=m.padded[:, NT - 1:NT], in_=m.padded[:, NT - 1:NT], compare_op=ALU.is_ge,
                               fill=1.0, base=TAIL - 1, pattern=[[0, 1]], channel_multiplier=-1
                               ).then_inc(s_made, 1)
            pool.affine_select(out=m.sel[:, :, :], in_=m.sel[:, :, :], compare_op=ALU.not_equal, fill=1.0,
                               base=0, pattern=[[-1, EX], [0, P]], channel_multiplier=1).then_inc(s_made, 1)

        @block.vector
        def _(dve):
            dve.memset(m.X[:, NT - 1, :], 0.0).then_inc(s_zeroed, 1)
            dve.wait_ge(s_made, 12)
            dve.tensor_copy(m.ruler[:, :], ruler_i[:, :])
            dve.tensor_copy(m.ident16[:, :], m.identf[:, :])
            for t in range(NT):
                if t == 0:
                    dve.wait_ge(s_nodes, 64)
                dve.bn_stats(m.stats[:, t, :], m.X[:, t, :])


def norm_scales(nc, m, twice=False):
    with ExitStack() as ctx:
        s = Stage(nc, m, ctx, "ns")
        (s_step, s_root) = s.signals(
            "step root")
        tmp = s.sb("tmp", [P, 3, NT])
        block = ctx.enter_context(nc.Block())

        @block.scalar
        def _(act):
            act.wait_ge(s_step, NT)
            act.activation(tmp[:, 0, :], m.mv[:, :, 1], ACT.Sqrt, bias=m.eps[:, 0:1]).then_inc(s_root, 1)
            if twice:
                act.wait_ge(s_step, NT + 3)
                act.activation(tmp[:, 2, :], tmp[:, 1, :], ACT.Sqrt, bias=m.eps[:, 0:1]).then_inc(s_root, 1)

        @block.vector
        def _(dve):
            for t in range(NT):
                dve.bn_aggr(m.mv[:, t, :], m.stats[:, t, :]).then_inc(s_step, 1)
            dve.wait_ge(s_root, 1)
            dve.reciprocal(m.scale[:, :], tmp[:, 0, :]).then_inc(s_step, 1)
            n = NT + 1
            dve.wait_ge(s_step, n)
            if twice:
                dve.tensor_tensor(tmp[:, 1, :], m.mv[:, :, 1], m.scale[:, :], ALU.mult).then_inc(s_step, 1)
                dve.wait_ge(s_step, n + 1)
                dve.tensor_tensor(tmp[:, 1, :], tmp[:, 1, :], m.scale[:, :], ALU.mult).then_inc(s_step, 1)
                dve.wait_ge(s_root, 2)
                dve.reciprocal(tmp[:, 2, :], tmp[:, 2, :]).then_inc(s_step, 1)
                dve.wait_ge(s_step, n + 3)
                dve.tensor_tensor(m.scale[:, :], m.scale[:, :], tmp[:, 2, :], ALU.mult).then_inc(s_step, 1)
                n += 4
                dve.wait_ge(s_step, n)
            dve.scalar_tensor_tensor(out=m.shift[:, :], in0=m.mv[:, :, 0], scalar=-1.0, in1=m.scale[:, :],
                                     op0=ALU.mult, op1=ALU.mult)


def count_edges(nc, m, io, ahead):
    with ExitStack() as ctx:
        s = Stage(nc, m, ctx, "ce")
        (s_blank, s_edges, s_cast, s_turned, s_cols, s_onehot, s_used, s_closed, s_drained, s_flipped,
         s_kept, s_tiles, s_plan, s_lined, s_row, s_far) = s.signals(
            "blank edges cast turned cols onehot used closed drained flipped kept tiles plan lined row far")
        raw = s.sb("raw", [P, 2, EG, P], I32)
        rawf = s.sb("rawf", [P, 2, EG, P])
        ends = s.sb("ends", [P, 2, EG * P])
        hot_d = s.sb("hot_d", [P, HOTS, P], F16)
        hot_s = s.sb("hot_s", [P, HOTS, N], F16)
        none = s.sb("none", [P, P], F16)
        tile_i = s.sb("tile_i", [P, EG], I32)
        tile_f = s.sb("tile_f", [P, EG])
        bounds = s.sb("bounds", [P, 2, EG])
        some = s.sb("some", [P, EG, P])
        plan = s.sb("plan", [P, 2, NT, EG])
        lined = s.sb("lined", [2 * NT, 1])
        row = s.sb("row", [1, 2 * NT + 1])
        row_i = s.sb("row_i", [1, 2 * NT + 1], I32)
        ps_e = s.psum("ps_e", [P, 2, BANK])
        ps_a = s.psum("ps_a", [P, 3 * BANK])
        ps_p = s.psum("ps_p", [2 * NT, BANK])
        ps_r = s.psum("ps_r", [1, BANK])
        block = ctx.enter_context(nc.Block())
        full = NE // P
        rest = NE - full * P
        last_g, last_p = full // P, full % P
        rounds = -(-ET // HOTS)

        @block.sync
        def _(sp):
            sp.wait_ge(s_blank, 1)
            for n, name in enumerate(("src", "dst")):
                e = io[name]
                for g in range(EG):
                    rows = min(P, full - g * P)
                    sp.dma_start(raw[0:rows, n, g, :], e[g * P * P:(g * P + rows) * P].rearrange(
                        "(t p) -> t p", p=P)).then_inc(s_edges, 16)
                sp.dma_start(raw[last_p:last_p + 1, n, last_g, 0:rest], e[full * P:NE].rearrange(
                    "(a p) -> a p", a=1)).then_inc(s_edges, 16)
            for dst, src in ahead[1]:
                sp.dma_start(dst, src).then_inc(ahead[0], 16)
            sp.wait_ge(ahead[0], 16 * len(ahead[1]))

        @block.gpsimd
        def _(pool):
            pool.iota(tile_i[:, :], [[P, EG]], base=0, channel_multiplier=1).then_inc(s_tiles, 1)

        @block.vector
        def _(dve):
            dve.memset(raw[:, :, :, :], -1).then_inc(s_blank, 1)
            dve.memset(none[:, :], 0.0).then_inc(s_blank, 1)
            dve.wait_ge(s_tiles, 1)
            dve.tensor_copy(tile_f[:, :], tile_i[:, :]).then_inc(s_plan, 1)
            dve.wait_ge(s_edges, 16 * 2 * (EG + 1))
            dve.tensor_copy(rawf[:, :, :, :], raw[:, :, :, :]).then_inc(s_cast, 1)
            dve.wait_ge(s_cast, 1)
            dve.tensor_reduce(bounds[:, 0, :], rawf[:, 1, :, :], AX_X, ALU.max).then_inc(s_plan, 1)
            dve.tensor_scalar(some[:, :, :], rawf[:, 1, :, :], 0.0, float(FAR), ALU.is_lt, ALU.mult
                              ).then_inc(s_plan, 1)
            dve.wait_ge(s_plan, 3)
            dve.tensor_tensor(some[:, :, :], some[:, :, :], rawf[:, 1, :, :], ALU.add).then_inc(s_plan, 1)
            dve.wait_ge(s_plan, 4)
            dve.tensor_reduce(bounds[:, 1, :], some[:, :, :], AX_X, ALU.min).then_inc(s_plan, 1)
            dve.wait_ge(s_plan, 5)
            for j in range(NT):
                dve.tensor_scalar(plan[:, 0, j, :], bounds[:, 0, :], float(j * P), float(FAR), ALU.is_lt, ALU.mult
                                  ).then_inc(s_far, 1)
                dve.tensor_scalar(plan[:, 1, j, :], bounds[:, 1, :], float((j + 1) * P), float(FAR), ALU.is_ge,
                                  ALU.mult).then_inc(s_far, 1)
            dve.wait_ge(s_far, 2 * NT)
            tiles = tile_f[:, :].unsqueeze(1).broadcast_to([P, NT, EG])
            dve.tensor_tensor(plan[:, 0, :, :], plan[:, 0, :, :], tiles, ALU.add).then_inc(s_plan, 1)
            dve.tensor_tensor(plan[:, 1, :, :], plan[:, 1, :, :], tiles, ALU.subtract).then_inc(s_plan, 1)
            dve.wait_ge(s_turned, 1)
            dve.tensor_copy(ends[:, :, :], ps_e[:, :, 0:EG * P]).then_inc(s_cols, 1)
            dve.wait_ge(s_lined, 1)
            dve.tensor_reduce(lined[:, :], ps_p[:, 0:EG * P], AX_X, ALU.min).then_inc(s_row, 1)
            dve.wait_ge(s_lined, 2)
            dve.tensor_copy(row[:, 0:2 * NT], ps_r[:, 0:2 * NT]).then_inc(s_row, 1)
            dve.wait_ge(s_row, 2)
            dve.tensor_tensor(row[:, NT:2 * NT], row[:, NT:2 * NT], row[:, 0:NT], ALU.add).then_inc(s_row, 1)
            dve.wait_ge(s_row, 3)
            dve.tensor_reduce(row[:, 2 * NT:2 * NT + 1], row[:, NT:2 * NT], AX_X, ALU.min).then_inc(s_row, 1)
            dve.wait_ge(s_row, 4)
            dve.tensor_scalar(row[:, 2 * NT:2 * NT + 1], row[:, 2 * NT:2 * NT + 1], float(1 - SPAN), None,
                              ALU.is_lt).then_inc(s_row, 1)
            dve.tensor_scalar(row[:, 0:NT], row[:, 0:NT], float(EG * P - SPAN), None, ALU.min).then_inc(s_row, 1)
            dve.wait_ge(s_row, 6)
            dve.tensor_copy(row_i[:, :], row[:, :]).then_inc(s_row, 1)
            dve.wait_ge(s_cols, 1)
            dve.wait_ge(s_row, 7)
            for opened in (s_onehot,):
                dve.sem_inc(opened, 1)

            def one_hots(count, all_tiles):
                with dve.Fori(0, NT) as j:
                    first = 0 if all_tiles else dve.value_load(row_i[0:1, bass.ds(j, 1)], min_val=0,
                                                               max_val=EG * P - SPAN)
                    with dve.Fori(0, count) as i:
                        for u in range(HOTS):
                            e = HOTS * i + u + first
                            dve.wait_ge(s_used, j * (HOTS * count) + HOTS * i + u + 1)
                            dve.tensor_scalar(hot_d[:, u, :], m.ruler[:, bass.ts(j, P)], ends[:, 1, bass.ds(e, 1)],
                                              None, ALU.is_equal)
                            dve.tensor_scalar(hot_s[:, u, :], m.ruler[:, 0:N], ends[:, 0, bass.ds(e, 1)], None,
                                              ALU.is_equal).then_inc(s_onehot, 1)

            scattered = dve.value_load(row_i[0:1, 2 * NT:2 * NT + 1], min_val=0, max_val=1)
            with dve.If(scattered):
                one_hots(rounds, True)
            with dve.Else():
                one_hots(SPAN // HOTS, False)

        @block.tensor
        def _(pe):
            pe.sem_inc(s_used, HOTS - 1)
            pe.wait_ge(s_cast, 1)
            for n in range(2):
                for g in range(EG):
                    mm = pe.transpose(ps_e[:, n, g * P:(g + 1) * P], rawf[:, n, g, :], m.identf[:, :])
            mm.then_inc(s_turned, 1)
            pe.wait_ge(s_plan, 7)
            for g in range(EG):
                mm = pe.transpose(ps_p[:, g * P:(g + 1) * P], plan[:, :, :, g].rearrange("p a j -> p (a j)"),
                                  m.identf[:, :])
            mm.then_inc(s_lined, 1)
            pe.wait_ge(s_row, 1)
            pe.transpose(ps_r[:, 0:2 * NT], lined[:, :], m.identf[0:2 * NT, 0:2 * NT]).then_inc(s_lined, 1)
            pe.wait_ge(s_cols, 1)
            pe.wait_ge(s_blank, 2)
            pe.wait_ge(s_row, 7)
            pe.matmul(ps_a[:, 0:P], none[:, :], none[:, :], start=True, stop=True).then_inc(s_used, 1)

            def products(count):
                with pe.Fori(0, NT) as j:
                    pe.wait_ge(s_drained, j + 1)
                    for a, w in pieces(NP):
                        pe.matmul(ps_a[:, a:a + w], none[:, :], m.ruler[:, a:a + w], start=True, stop=False)
                    with pe.Fori(0, count) as i:
                        for u in range(HOTS):
                            pe.wait_ge(s_onehot, j * (HOTS * count) + HOTS * i + u + 2)
                            for a, w in pieces(N):
                                mm = pe.matmul(ps_a[:, a:a + w], hot_d[:, u, :], hot_s[:, u, a:a + w],
                                               start=False, stop=False)
                            mm.then_inc(s_used, 1)
                    for a, w in pieces(NP):
                        mm = pe.matmul(ps_a[:, a:a + w], none[:, :], m.ruler[:, a:a + w], start=False, stop=True)
                    mm.then_inc(s_closed, 1)

            scattered = pe.value_load(row_i[0:1, 2 * NT:2 * NT + 1], min_val=0, max_val=1)
            with pe.If(scattered):
                products(rounds)
            with pe.Else():
                products(SPAN // HOTS)
            pe.wait_ge(s_drained, NT + 1)
            with pe.Fori(0, NT) as j:
                pe.wait_ge(s_kept, j + 1)
                for b in range(NT):
                    mm = pe.matmul(ps_a[:, b * P:(b + 1) * P], m.A[:, b, bass.ts(j, P)], m.ident16[:, :],
                                   start=True, stop=True)
                mm.then_inc(s_flipped, 1)

        @block.scalar
        def _(act):
            for opened in (s_drained, s_kept):
                act.sem_inc(opened, 1)
            with act.Fori(0, NT) as j:
                act.wait_ge(s_closed, j + 1)
                act.activation(m.A[:, bass.ds(j, 1), :], ps_a[:, 0:NP], ACT.Copy,
                               accum_out=m.deg_d[:, bass.ds(j, 1)]).then_inc(s_drained, 1)
            with act.Fori(0, NT) as j:
                act.wait_ge(s_flipped, j + 1)
                act.activation(m.AT[:, bass.ds(j, 1), :], ps_a[:, 0:NP], ACT.Copy,
                               accum_out=m.deg_s[:, bass.ds(j, 1)]).then_inc(s_kept, 1)


def node_rows(nc, m, xn, hi, lo):
    with ExitStack() as ctx:
        s = Stage(nc, m, ctx, "nr")
        (s_rows, s_high) = s.signals(
            "rows high")
        block = ctx.enter_context(nc.Block())

        @block.scalar
        def _(act):
            for t in range(NT):
                act.activation(xn[:, t, :], m.X[:, t, :], ACT.Identity, bias=m.shift[:, t:t + 1],
                               scale=m.scale[:, t:t + 1]).then_inc(s_rows, 1)

        @block.vector
        def _(dve):
            for t in range(NT):
                dve.wait_ge(s_rows, t + 1)
                dve.tensor_copy(hi[:, t, :], xn[:, t, :]).then_inc(s_high, 1)

        @block.gpsimd
        def _(pool):
            for t in range(NT):
                pool.wait_ge(s_high, t + 1)
                pool.tensor_tensor(lo[:, t, :], xn[:, t, :], hi[:, t, :], ALU.subtract)


def aggregate(nc, m, hi, lo, adj, agg):
    with ExitStack() as ctx:
        s = Stage(nc, m, ctx, "ag")
        (s_summed, s_kept_v, s_kept_a) = s.signals(
            "summed kept_v kept_a")
        ps = s.psum("ps", [P, KD, BANK])
        block = ctx.enter_context(nc.Block())

        @block.tensor
        def _(pe):
            with pe.Fori(0, NCH) as c:
                for f in range(KD):
                    pe.wait_ge(s_kept_a if f % 2 else s_kept_v, 2 * c + 1)
                    for t in range(NT):
                        for part in (hi, lo):
                            mm = pe.matmul(ps[:, f, 0:CH], part[:, t, f * P:(f + 1) * P],
                                           adj[:, t, bass.ts(c, CH)],
                                           start=(t == 0 and part is hi), stop=(t == NT - 1 and part is lo))
                    mm.then_inc(s_summed, 1)

        @block.vector
        def _(dve):
            for opened in (s_kept_v,):
                dve.sem_inc(opened, 1)
            with dve.Fori(0, NCH) as c:
                for f in (0, 2):
                    dve.wait_ge(s_summed, KD * c + f + 1)
                    dve.tensor_copy(agg[:, f, bass.ts(c, CH)], ps[:, f, 0:CH]).then_inc(s_kept_v, 1)

        @block.scalar
        def _(act):
            for opened in (s_kept_a,):
                act.sem_inc(opened, 1)
            with act.Fori(0, NCH) as c:
                for f in (1, 3):
                    act.wait_ge(s_summed, KD * c + f + 1)
                    act.copy(agg[:, f, bass.ts(c, CH)], ps[:, f, 0:CH]).then_inc(s_kept_a, 1)


def graph_rows(nc, m, xn, agg, w_own, w_near, deg, bias, affine=None):
    with ExitStack() as ctx:
        s = Stage(nc, m, ctx, "gr")
        (s_inv, s_rows_in, s_near_in, s_cols, s_own_done, s_near_done, s_step, s_free_ps, s_free_t,
         s_root, s_passed) = s.signals(
            "inv rows_in near_in cols own_done near_done step free_ps free_t root passed")
        xs = s.sb("xs", [P, 2, D])
        near = s.sb("near", [P, 2, KD, P])
        xt = s.sb("xt", [P, 2, KD, P])
        hsum = s.sb("hsum", [P, 2, D])
        st = s.sb("st", [P, 2, 6])
        mv = s.sb("mvh", [P, 2, 2])
        sc = s.sb("sc", [P, 2, 3])
        inv = s.sb("inv", [P, NT])
        ps_t = s.psum("ps_t", [P, 2, KD, P])
        ps_n = s.psum("ps_n", [P, 2, BANK])
        ps_o = s.psum("ps_o", [P, 2, BANK])
        block = ctx.enter_context(nc.Block())

        @block.gpsimd
        def _(pool):
            with pool.Fori(0, NT // 2) as i:
                for u in range(2):
                    pool.wait_ge(s_free_t, 2 * i + 1)
                    pool.tensor_copy(xs[:, u, :], xn[:, bass.ds(2 * i + u, 1), :]).then_inc(s_rows_in, 1)

        @block.scalar
        def _(act):
            with act.Fori(0, NT // 2) as i:
                for u in range(2):
                    t = 2 * i + u
                    act.wait_ge(s_near_done, 2 * i + 1)
                    act.copy(near[:, u, :, :], agg[:, :, bass.ts(t, P)]).then_inc(s_near_in, 1)
                    if affine:
                        act.wait_ge(s_step, 9 * t + 4)
                        act.activation(sc[:, u, 0:1], mv[:, u, 1:2], ACT.Sqrt, bias=m.eps[:, 0:1]
                                       ).then_inc(s_root, 1)

        @block.tensor
        def _(pe):
            for opened in (s_free_t, s_near_done, s_own_done):
                pe.sem_inc(opened, 1)
            with pe.Fori(0, NT // 2) as i:
                for u in range(2):
                    t = 2 * i + u
                    pe.wait_ge(s_rows_in, t + 1)
                    pe.wait_ge(s_cols, 2 * i + 1)
                    for k in range(KD):
                        mm = pe.transpose(ps_t[:, u, k, :], xs[:, u, k * P:(k + 1) * P], m.identf[:, :])
                    mm.then_inc(s_free_t, 1)
                    pe.wait_ge(s_near_in, t + 1)
                    pe.wait_ge(s_free_ps, 2 * i + 1)
                    for k in range(KD):
                        mm = pe.matmul(ps_n[:, u, :], near[:, u, k, :], w_near[:, k, :],
                                       start=(k == 0), stop=(k == KD - 1))
                    mm.then_inc(s_near_done, 1)
                    pe.wait_ge(s_cols, t + 2)
                    for k in range(KD):
                        mm = pe.matmul(ps_o[:, u, :], xt[:, u, k, :], w_own[:, k, :],
                                       start=(k == 0), stop=(k == KD - 1))
                    mm.then_inc(s_own_done, 1)

        @block.vector
        def _(dve):
            for opened in (s_cols, s_free_ps):
                dve.sem_inc(opened, 1)
            dve.tensor_tensor(inv[:, :], deg[:, :], m.padded[:, :], ALU.add).then_inc(s_inv, 1)
            n = 1
            if affine:
                dve.wait_ge(s_inv, 1)
                dve.tensor_scalar(inv[:, :], inv[:, :], 1.0, None, ALU.max).then_inc(s_inv, 1)
                n = 2
            dve.wait_ge(s_inv, n)
            dve.reciprocal(inv[:, :], inv[:, :]).then_inc(s_inv, 1)
            dve.wait_ge(s_inv, n + 1)
            c = 9 if affine else 3
            with dve.Fori(0, NT // 2) as i:
                for u in range(2):
                    t = 2 * i + u
                    hs, x_t = hsum[:, u, :], m.X[:, bass.ds(t, 1), :]
                    dve.wait_ge(s_free_t, t + 2)
                    dve.wait_ge(s_own_done, 2 * i + 1)
                    dve.tensor_copy(xt[:, u, :, :], ps_t[:, u, :, :]).then_inc(s_cols, 1)
                    dve.wait_ge(s_near_done, t + 2)
                    dve.scalar_tensor_tensor(out=hs, in0=ps_n[:, u, :], scalar=inv[:, bass.ds(t, 1)],
                                             in1=bias[:, :], op0=ALU.mult, op1=ALU.add).then_inc(s_step, 1)
                    dve.wait_ge(s_own_done, t + 2)
                    dve.wait_ge(s_step, c * t + 1)
                    dve.tensor_tensor(hs, hs, ps_o[:, u, :], ALU.add).then_inc(s_step, 1)
                    dve.wait_ge(s_step, c * t + 2)
                    if affine:
                        dve.bn_stats(st[:, u, :], hs).then_inc(s_step, 1)
                        dve.wait_ge(s_step, c * t + 3)
                        dve.sem_inc(s_passed, 1)
                        dve.bn_aggr(mv[:, u, :], st[:, u, :]).then_inc(s_step, 1)
                        dve.wait_ge(s_root, t + 1)
                        dve.reciprocal(sc[:, u, 1:2], sc[:, u, 0:1]).then_inc(s_step, 1)
                        dve.wait_ge(s_step, c * t + 5)
                        dve.tensor_scalar(hs, hs, mv[:, u, 0:1], sc[:, u, 1:2],
                                          ALU.subtract, ALU.mult).then_inc(s_step, 1)
                        dve.wait_ge(s_step, c * t + 6)
                        dve.tensor_tensor(hs, hs, affine[0][:, :], ALU.mult).then_inc(s_step, 1)
                        dve.wait_ge(s_step, c * t + 7)
                        dve.tensor_tensor(hs, hs, affine[1][:, :], ALU.add).then_inc(s_step, 1)
                        dve.wait_ge(s_step, c * t + 8)
                    dve.tensor_tensor(x_t, x_t, hsum[:, u:u + 1, :], ALU.add).then_inc(s_step, 1)
                    dve.wait_ge(s_step, c * t + c)
                    dve.bn_stats(m.stats[:, bass.ds(t, 1), :], x_t).then_inc(s_free_ps, 1)


def turn_weights(nc, m, raws, outs):
    with ExitStack() as ctx:
        s = Stage(nc, m, ctx, "tw")
        (s_turned, s_kept) = s.signals(
            "turned kept")
        ps = s.psum("ps", [P, 2, KD, P])
        block = ctx.enter_context(nc.Block())
        work = [(raw, out, b) for raw, out in zip(raws, outs) for b in range(raw.shape[1])]

        @block.tensor
        def _(pe):
            for n, (raw, out, b) in enumerate(work):
                if n >= 2:
                    pe.wait_ge(s_kept, n - 1)
                for k in range(KD):
                    mm = pe.transpose(ps[:, n % 2, k, :], raw[:, b, k * P:(k + 1) * P], m.identf[:, :])
                mm.then_inc(s_turned, 1)

        @block.vector
        def _(dve):
            for n, (raw, out, b) in enumerate(work):
                dve.wait_ge(s_turned, n + 1)
                dve.tensor_copy(out[:, :, b * P:(b + 1) * P], ps[:, n % 2, :, :]).then_inc(s_kept, 1)


def causal_qkv(nc, m, io, QO, KT, V):
    with ExitStack() as ctx:
        s = Stage(nc, m, ctx, "cq")
        (s_wts, s_rows, s_turned, s_cols, s_q_ps, s_k_ps, s_v_ps, s_v_kept, s_sq, s_summed, s_root,
         s_step, s_qk_turned, s_q_kept, s_k_kept, s_gained) = s.signals(
            "wts rows turned cols q_ps k_ps v_ps v_kept sq summed root step qk_turned "
            "q_kept k_kept gained")
        wq = s.sb("wq", [P, KD, D])
        wk = s.sb("wk", [P, KD, D])
        wv = s.sb("wv", [P, KD, D])
        gains = s.sb("gains", [P, 2 * KD + 2])
        hn = s.sb("hn", [P, 2, D])
        ht = s.sb("ht", [P, 2, KD, P])
        sq = s.sb("sq", [P, 2, D])
        ss = s.sb("ss", [P, 3, 2, H])
        qn = s.sb("qn", [P, 2, D])
        ps_t = s.psum("ps_t", [P, 2, KD, P])
        ps_q = s.psum("ps_q", [P, 2, BANK])
        ps_v = s.psum("ps_v", [P, BANK])
        ps_r = s.psum("ps_r", [P, 2, KD, P])
        block = ctx.enter_context(nc.Block())

        @block.sync
        def _(sp):
            for w, name in ((wq, "L0_ffn_Wq"), (wk, "L0_ffn_Wk"), (wv, "L0_ffn_Wv")):
                sp.dma_start(w[:, :, :], io[name].rearrange("(k p) n -> p k n", p=P)).then_inc(s_wts, 16)
            for c, name in ((0, "L0_ffn_ln_g"), (KD, "L0_ffn_ln_b")):
                sp.dma_start(gains[:, c:c + KD], io[name].rearrange("(k p) -> p k", p=P)).then_inc(s_wts, 16)
            for c, name in ((2 * KD, "L0_ffn_qn_g"), (2 * KD + 1, "L0_ffn_kn_g")):
                for half in range(2):
                    sp.dma_start(gains[half * DH:(half + 1) * DH, c:c + 1],
                                 io[name].rearrange("(p a) -> p a", a=1)).then_inc(s_wts, 16)
            sp.wait_ge(s_wts, 16 * 9)

        @block.scalar
        def _(act):
            for opened in (s_v_kept, s_q_kept, s_k_kept, s_root):
                act.sem_inc(opened, 1)
            act.wait_ge(s_wts, 16 * 9)
            act.wait_ge(s_gained, 1)
            with act.Fori(0, NT // 2) as i:
                for u in range(2):
                    t = 2 * i + u
                    act.wait_ge(s_turned, 2 * i + 1)
                    act.activation(hn[:, u, :], m.X[:, bass.ds(t, 1), :], ACT.Identity,
                                   bias=m.shift[:, bass.ds(t, 1)], scale=m.scale[:, bass.ds(t, 1)]
                                   ).then_inc(s_rows, 1)
                    for n, done in enumerate((s_q_ps, s_k_ps)):
                        act.wait_ge(done, t + 1)
                        act.wait_ge(s_summed, 2 * t + 1)
                        act.activation(sq[:, n, :], ps_q[:, n, :], ACT.Square).then_inc(s_sq, 1)
                    act.wait_ge(s_v_ps, t + 2)
                    act.copy(V[:, bass.ds(t, 1), :].rearrange("p t (h c) -> p (t h) c", h=H)[:, :, 0:DH],
                             ps_v[:, :].rearrange("p (h c) -> p h c", h=H)).then_inc(s_v_kept, 1)
                    act.wait_ge(s_summed, 2 * t + 3)
                    act.activation(ss[:, 1, :, :], ss[:, 0, :, :], ACT.Sqrt, bias=m.eps[:, 1:2]).then_inc(s_root, 1)
                    act.wait_ge(s_qk_turned, 2 * t + 2)
                    act.activation(QO[:, :, bass.ts(t, P)], ps_r[:, 0, :, :], ACT.Copy,
                                   scale=gains[:, 2 * KD:2 * KD + 1]).then_inc(s_q_kept, 1)
                    act.wait_ge(s_qk_turned, 2 * t + 3)
                    act.activation(KT[:, :, bass.ts(t, P)], ps_r[:, 1, :, :], ACT.Copy,
                                   scale=gains[:, 2 * KD + 1:2 * KD + 2]).then_inc(s_k_kept, 1)

        @block.vector
        def _(dve):
            for opened in (s_summed, s_cols, s_step):
                dve.sem_inc(opened, 1)
            dve.wait_ge(s_wts, 16 * 9)
            dve.tensor_scalar(gains[:, 2 * KD + 1:2 * KD + 2], gains[:, 2 * KD + 1:2 * KD + 2], float(DH) ** 0.5,
                              None, ALU.mult).then_inc(s_gained, 1)
            with dve.Fori(0, NT // 2) as i:
                for u in range(2):
                    t = 2 * i + u
                    dve.wait_ge(s_turned, t + 2)
                    dve.wait_ge(s_v_ps, 2 * i + 1)
                    for k in range(KD):
                        ins = dve.tensor_scalar(ht[:, u, k, :], ps_t[:, u, k, :], gains[:, k:k + 1],
                                                gains[:, KD + k:KD + k + 1], ALU.mult, ALU.add)
                    ins.then_inc(s_cols, 1)
                    for n in range(2):
                        dve.wait_ge(s_sq, 2 * t + n + 1)
                        if n == 0:
                            dve.wait_ge(s_root, t + 1)
                        dve.tensor_reduce(ss[:, 0, n, :], sq[:, n, :].rearrange("p (h d) -> p h d", h=H),
                                          AX_X, ALU.add).then_inc(s_summed, 1)
                    dve.wait_ge(s_root, t + 2)
                    dve.reciprocal(ss[:, 2, :, :], ss[:, 1, :, :]).then_inc(s_step, 1)
                    dve.wait_ge(s_step, 3 * t + 2)
                    for n in range(2):
                        dve.wait_ge(s_qk_turned, 2 * t + n + 1)
                        dve.tensor_tensor(qn[:, n, :].rearrange("p (h d) -> p h d", h=H),
                                          ps_q[:, n, :].rearrange("p (h d) -> p h d", h=H),
                                          ss[:, 2, n, :].unsqueeze(2).broadcast_to([P, H, DH]), ALU.mult
                                          ).then_inc(s_step, 1)

        @block.gpsimd
        def _(pool):
            pool.memset(V[:, :, :].rearrange("p t (h c) -> p (t h) c", h=H)[:, :, DH:DH + 1], 1.0)

        @block.tensor
        def _(pe):
            for opened in (s_turned, s_qk_turned, s_v_ps):
                pe.sem_inc(opened, 1)
            pe.wait_ge(s_wts, 16 * 9)
            with pe.Fori(0, NT // 2) as i:
                for u in range(2):
                    t = 2 * i + u
                    pe.wait_ge(s_rows, t + 1)
                    pe.wait_ge(s_cols, 2 * i + 1)
                    for k in range(KD):
                        mm = pe.transpose(ps_t[:, u, k, :], hn[:, u, k * P:(k + 1) * P], m.identf[:, :])
                    mm.then_inc(s_turned, 1)
                    pe.wait_ge(s_cols, t + 2)
                    pe.wait_ge(s_step, 3 * t + 1)
                    for w, ps, done in ((wq, ps_q[:, 0, :], s_q_ps), (wk, ps_q[:, 1, :], s_k_ps),
                                        (wv, ps_v[:, :], s_v_ps)):
                        if w is wv:
                            pe.wait_ge(s_v_kept, t + 1)
                        for k in range(KD):
                            mm = pe.matmul(ps, ht[:, u, k, :], w[:, k, :], start=(k == 0), stop=(k == KD - 1))
                        mm.then_inc(done, 1)
                    for n, kept in enumerate((s_q_kept, s_k_kept)):
                        pe.wait_ge(s_step, 3 * t + 2 + n + 1)
                        pe.wait_ge(kept, t + 1)
                        for k in range(KD):
                            mm = pe.transpose(ps_r[:, n, k, :], qn[:, n, k * P:(k + 1) * P], m.identf[:, :])
                        mm.then_inc(s_qk_turned, 1)


def attention(nc, m, QO, KT, V, top, ahead=None):
    SN = 2 * NT

    def place(n):
        n = n % SN
        width = NP if top else (n % NT + 1) * P
        return n // NT, n % NT, width, pieces(width)

    before = [0]
    for n in range(2 * SN):
        before.append(before[-1] + len(place(n)[3]))
    GN = before[SN]
    with ExitStack() as ctx:
        s = Stage(nc, m, ctx, "at")
        (s_fetched_0, s_fetched_1, s_cut_passed, s_staged, s_scored, s_exp, s_masked, s_maxed, s_turned,
         s_kept, s_o_done, s_o_kept, s_step) = s.signals(
            "fetched_0 fetched_1 cut_passed staged scored exp masked maxed turned "
            "kept o_done o_kept step")
        if top:
            (s_read, s_topped, s_rest, s_probs, s_passed) = s.signals(
                "read topped rest probs passed")
        qs = s.sb("qs", [P, 2, NP], F32R)
        kh = s.sb("kh", [P, 2, NP], F32R)
        kl = s.sb("kl", [P, 2, NP], F32R)
        qh = s.sb("qh", [P, NP], F32R)
        ex = s.sb("ex", [P, 2, NP])
        pt = s.sb("pt", [P, 2, NP])
        negm = s.sb("negm", [P, 2])
        rsum = s.sb("rsum", [P, 2])
        if top:
            left = s.sb("left", [P, 2, N])
            m8 = s.sb("m8", [P, 2, 8])
        ps_s = [s.psum(f"ps_s{b}", [P, 3 * BANK]) for b in range(2)]
        ps_t = s.psum("ps_t", [P, BANK])
        ps_o = s.psum("ps_o", [P, BANK])
        block = ctx.enter_context(nc.Block())

        def each_pair(eng, program):
            with eng.Fori(0, HP - 1) as i:
                program(i, False)
            program(HP - 1, True)

        s_fetched = (s_fetched_0, s_fetched_1)

        @block.sync
        def _(sp):
            def fetch(i, half):
                r = slice(half * DH, (half + 1) * DH)
                for arrived, rows in ((qs, QO), (kl, KT)):
                    for to in range(2):
                        sp.dma_start(arrived[to * DH:(to + 1) * DH, half:half + 1, :].bitcast(F32),
                                     rows[r, bass.ds(i, 1), :]).then_inc(s_fetched[half], 16)

            fetch(0, 0)
            fetch(0, 1)
            if ahead:
                for dst, src in ahead[1]:
                    sp.dma_start(dst, src).then_inc(ahead[0], 16)
            with sp.Fori(0, HP - 1) as i:
                for half in range(2):
                    sp.wait_ge(s_scored, SN * i + (half + 1) * NT + 1)
                    fetch(i + 1, half)
            for half in range(2):
                sp.wait_ge(s_fetched[half], 64 * HP)
            if ahead:
                sp.wait_ge(ahead[0], 16 * len(ahead[1]))

        @block.gpsimd
        def _(pool):
            def stage(i, half, step):
                upper, lower = slice(0, DH), slice(DH, P)
                if step == 0:
                    pool.wait_ge(s_fetched[half], 64 * i + 64)
                pool.sem_inc(s_cut_passed, 1)
                if step == 0:
                    op = pool.tensor_copy(kh[:, half, :], kl[:, half, :].bitcast(F32))
                elif step == 1:
                    op = pool.tensor_tensor(kl[:, half, :], kl[:, half, :].bitcast(F32),
                                            kh[:, half, :].bitcast(F32), ALU.subtract)
                elif step == 2:
                    op = pool.tensor_copy(qh[lower, :], qs[lower, half, :].bitcast(F32))
                elif step == 3:
                    op = pool.tensor_tensor(qs[lower, half, :], qs[lower, half, :].bitcast(F32),
                                            qh[lower, :].bitcast(F32), ALU.subtract)
                else:
                    op = pool.tensor_copy(qs[upper, half, :], qs[upper, half, :].bitcast(F32))
                op.then_inc(s_staged, 1)
                pool.wait_ge(s_staged, 5 * (2 * i + half) + step + 1)

            def subtract(i, n):
                pool.wait_ge(s_rest, SN * i + n + 2)
                pool.tensor_tensor(ex[:, n % 2, 0:N], ex[:, n % 2, 0:N], left[:, n % 2, :], ALU.subtract
                                   ).then_inc(s_probs, 1)
                pool.wait_ge(s_probs, SN * i + n + 2)

            def pair(i, last):
                for n in range(SN):
                    if top:
                        subtract(i, n)
                    if 2 <= n < 7:
                        stage(i, 1, n - 2)
                    if not last and NT + 2 <= n < NT + 7:
                        stage(i + 1, 0, n - NT - 2)

            if top:
                pool.memset(ex[:, :, N:NP], 0.0).then_inc(s_probs, 1)
                pool.wait_ge(s_probs, 1)
            for step in range(5):
                stage(0, 0, step)
            each_pair(pool, pair)

        @block.tensor
        def _(pe):
            for opened in (s_scored, s_o_done, s_turned):
                pe.sem_inc(opened, 1)

            def scores(i, n):
                half, t, width, parts = place(n)
                pe.wait_ge(s_staged, 10 * (i + n // SN) + 5 * half + 5)
                pe.wait_ge(s_exp, SN * i + max(n - 1, 0) + 1)
                if top:
                    pe.wait_ge(s_read, SN * i + max(n - 1, 0) + 1)
                for part in (kh, kl):
                    for a, w in parts:
                        mm = pe.matmul(ps_s[n % 2][:, a:a + w], qs[:, half, t * P:(t + 1) * P],
                                       part[:, half, a:a + w], start=(part is kh), stop=(part is kl))
                mm.then_inc(s_scored, 1)

            def turn(i, n, g):
                c = before[n] + g
                if g == 0:
                    pe.wait_ge(s_probs if top else s_exp, SN * i + n + 2)
                pe.wait_ge(s_kept, GN * i + c + 1)
                a, w = place(n)[3][g]
                for b in range(w // P):
                    mm = pe.transpose(ps_t[:, b * P:(b + 1) * P], ex[:, n % 2, a + b * P:a + (b + 1) * P],
                                      m.identf[:, :])
                mm.then_inc(s_turned, 1)

            def weigh(i, n, g):
                half, t, width, parts = place(n)
                pe.wait_ge(s_kept, GN * i + before[n] + g + 2)
                if g == 0:
                    pe.wait_ge(s_o_kept, SN * i + n + 1)
                a, w = parts[g]
                for k in range(a // P, (a + w) // P):
                    mm = pe.matmul(ps_o[:, 0:DH + 1], pt[:, n % 2, k * P:(k + 1) * P],
                                   V[:, k, bass.ds((2 * i + half) * (DH + 1), DH + 1)],
                                   start=(k == 0), stop=(k == width // P - 1))
                if g == len(parts) - 1:
                    mm.then_inc(s_o_done, 1)

            def pair(i, last):
                for n in range(SN):
                    parts = place(n)[3]
                    if not top:
                        turn(i, n, 0)
                    if not last or n + 2 < SN:
                        scores(i, n + 2)
                    if top:
                        turn(i, n, 0)
                    for g in range(1, len(parts)):
                        turn(i, n, g)
                        weigh(i, n, g - 1)
                    weigh(i, n, len(parts) - 1)

            scores(0, 0)
            scores(0, 1)
            each_pair(pe, pair)

        @block.scalar
        def _(act):
            for opened in (s_exp, s_kept) + ((s_rest,) if top else ()):
                act.sem_inc(opened, 1)

            def exponentials(i, n):
                width = place(n)[2] if not top else N
                act.wait_ge(s_maxed, SN * i + n + 1)
                if top:
                    act.wait_ge(s_read, SN * i + n + 2)
                act.wait_ge(s_turned, GN * i + before[max(n - 1, 0)] + 1)
                act.activation(ex[:, n % 2, 0:width], ps_s[n % 2][:, 0:width], ACT.Exp,
                               bias=negm[:, n % 2:n % 2 + 1]).then_inc(s_exp, 1)

            def rest(i, n):
                if top:
                    act.wait_ge(s_topped, SN * i + n + 2)
                    act.activation(left[:, n % 2, :], left[:, n % 2, :], ACT.Exp, bias=negm[:, n % 2:n % 2 + 1]
                                   ).then_inc(s_rest, 1)

            def keep(i, n):
                for g, (a, w) in enumerate(place(n)[3]):
                    act.wait_ge(s_turned, GN * i + before[n] + g + 2)
                    if g == 0:
                        act.wait_ge(s_o_done, SN * i + max(n - 1, 0) + 1)
                    act.copy(pt[:, n % 2, a:a + w], ps_t[:, 0:w]).then_inc(s_kept, 1)

            def pair(i, last):
                for n in range(SN):
                    if not last or n + 1 < SN:
                        if top:
                            rest(i, n + 1)
                        else:
                            exponentials(i, n + 1)
                    keep(i, n)
                    if top and (not last or n + 2 < SN):
                        exponentials(i, n + 2)

            exponentials(0, 0)
            if top:
                rest(0, 0)
                exponentials(0, 1)
            each_pair(act, pair)

        @block.vector
        def _(dve):
            for opened in (s_o_kept,) + ((s_topped, s_read) if top else ()):
                dve.sem_inc(opened, 1)

            def largest(i, n):
                half, t, width, parts = place(n)
                nm = negm[:, n % 2:n % 2 + 1]
                count = SN * i + n
                logits = ps_s[n % 2]
                dve.wait_ge(s_scored, count + 2)
                if not top:
                    own = logits[:, t * P:(t + 1) * P]
                    dve.tensor_tensor(own, own, m.causal[:, :], ALU.add).then_inc(s_masked, 1)
                    dve.wait_ge(s_masked, count + 1)
                    dve.wait_ge(s_exp, SN * i + max(n - 1, 0) + 1)
                    dve.tensor_reduce(nm, logits[:, 0:width], AX_X, ALU.max, negate=True).then_inc(s_maxed, 1)
                    return
                dve.sem_inc(s_passed, 1)
                dve.max(m8[:, 0, :], logits[:, 0:N]).then_inc(s_masked, 1)
                dve.wait_ge(s_masked, 2 * count + 1)
                dve.wait_ge(s_rest, SN * i + max(n - 1, 0) + 1)
                dve.tensor_scalar(nm, m8[:, 0, 0:1], -1.0, None, ALU.mult).then_inc(s_maxed, 1)
                dve.wait_ge(s_probs, SN * i + max(n - 1, 0) + 1)
                dve.sem_inc(s_passed, 1)
                dve.match_replace(left[:, n % 2, :], m8[:, 0, :], logits[:, 0:N], TAKEN).then_inc(s_read, 1)
                dve.wait_ge(s_read, count + 2)
                dve.wait_ge(s_topped, count + 1)
                dve.wait_ge(s_maxed, count + 1)
                dve.sem_inc(s_passed, 1)
                dve.max(m8[:, 1, :], left[:, n % 2, :]).then_inc(s_masked, 1)
                dve.wait_ge(s_masked, 2 * count + 2)
                dve.sem_inc(s_passed, 1)
                dve.match_replace(left[:, n % 2, :], m8[:, 1, :], left[:, n % 2, :], TAKEN).then_inc(s_topped, 1)

            def divide(i, n):
                half, t = place(n)[0:2]
                dve.wait_ge(s_o_done, SN * i + n + 2)
                if n == 0:
                    for h in range(2):
                        dve.wait_ge(s_fetched[h], 64 * i + 64)
                dve.wait_ge(s_o_kept, SN * i + max(n - 1, 0) + 1)
                dve.reciprocal(rsum[:, n % 2:n % 2 + 1], ps_o[:, DH:DH + 1]).then_inc(s_step, 1)
                dve.wait_ge(s_step, SN * i + n + 1)
                dve.tensor_scalar(QO[:, bass.ds(i, 1), t * P + half * DH:t * P + (half + 1) * DH],
                                  ps_o[:, 0:DH], rsum[:, n % 2:n % 2 + 1], None, ALU.mult).then_inc(s_o_kept, 1)

            ahead = 2

            def pair(i, last):
                for n in range(SN):
                    if not last or n + ahead < SN:
                        largest(i, n + ahead)
                    divide(i, n)

            for n in range(ahead):
                largest(0, n)
            each_pair(dve, pair)


def experts(nc, m, io, QO, w1_first, w1_last, w2):
    with ExitStack() as ctx:
        s = Stage(nc, m, ctx, "ex")
        (s_small, s_w1, s_w2, s_rows, s_turned, s_cols, s_y_ps, s_y_kept, s_logits, s_expd, s_step, s_gate,
         s_gate_t, s_gate_row, s_spread, s_hid, s_gelu, s_mixed, s_out, s_added) = s.signals(
            "small w1 w2 rows turned cols y_ps y_kept logits expd step gate gate_t gate_row "
            "spread hid gelu mixed out added")
        wo = s.sb("wo", [P, KD, D])
        gw = s.sb("gw", [P, KD, EX])
        gb = s.sb("gb", [1, EX])
        b1 = s.sb("b1", [P, FB])
        b2 = s.sb("b2", [EX, D])
        os_ = s.sb("os_", [P, 2, KD, P])
        ot = s.sb("ot", [P, 2, KD, P])
        yt = s.sb("yt", [P, 2, KD, P])
        hid = s.sb("hid", [P, FB, P])
        g = s.sb("g", [P, 4, EX])
        gt = s.sb("gt", [EX, P])
        ps_t = s.psum("ps_t", [P, KD, P])
        ps_y = s.psum("ps_y", [P, KD, P])
        ps_g = s.psum("ps_g", [P, BANK])
        ps_b = s.psum("ps_b", [P, EX, P])
        ps_h = s.psum("ps_h", [P, 2, 4, P])
        ps_x = s.psum("ps_x", [P, BANK])
        block = ctx.enter_context(nc.Block())
        QB = FB // 4

        @block.sync
        def _(sp):
            sp.dma_start(wo[:, :, :], io["L0_ffn_Wo"].rearrange("(k p) n -> p k n", p=P)).then_inc(s_small, 16)
            sp.dma_start(gw[:, :, :], io["L0_ffn_gate_W"].rearrange("(k p) e -> p k e", p=P)).then_inc(s_small, 16)
            sp.dma_start(gb[:, :], io["L0_ffn_gate_b"].rearrange("(a e) -> a e", a=1)).then_inc(s_small, 16)
            sp.dma_start(b1[:, :], io["L0_ffn_b1"].rearrange("e (b p) -> p (e b)", p=P)).then_inc(s_small, 16)
            sp.dma_start(b2[:, :], io["L0_ffn_b2"]).then_inc(s_small, 16)
            for e in range(EARLY, EX):
                c = (e - EARLY) * FF
                sp.dma_start(w1_last[:, :, c:c + FF], rows_of(io["L0_ffn_W1"][e])).then_inc(s_w1, 16)
            w2_rows = io["L0_ffn_W2"].rearrange("e (b p) n -> p (e b) n", p=P)
            for a in range(0, FB, FB // 2):
                sp.dma_start(w2[:, a:a + FB // 2, :], w2_rows[:, a:a + FB // 2, :]).then_inc(s_w2, 16)
            sp.wait_ge(s_small, 80)

        @block.gpsimd
        def _(pool):
            with pool.Fori(0, NT // 2) as i:
                for u in range(2):
                    t = 2 * i + u
                    pool.wait_ge(s_turned, 2 * i + 1)
                    pool.tensor_copy(os_[:, u, :, :], QO[:, :, bass.ts(t, P)]).then_inc(s_rows, 1)

        @block.tensor
        def _(pe):
            for opened in (s_turned, s_out, s_y_ps, s_gate_t):
                pe.sem_inc(opened, 1)
            pe.wait_ge(s_small, 80)
            with pe.Fori(0, NT // 2) as i:
                for u in range(2):
                    t = 2 * i + u
                    pe.wait_ge(s_rows, t + 1)
                    pe.wait_ge(s_cols, t + 1)
                    for k in range(KD):
                        mm = pe.transpose(ps_t[:, k, :], os_[:, u, k, :], m.identf[:, :])
                    mm.then_inc(s_turned, 1)
                    pe.wait_ge(s_cols, t + 2)
                    pe.wait_ge(s_y_kept, t + 1)
                    for f in range(KD):
                        for k in range(KD):
                            mm = pe.matmul(ps_y[:, f, :], wo[:, k, f * P:(f + 1) * P], ot[:, u, k, :],
                                           start=(k == 0), stop=(k == KD - 1))
                    mm.then_inc(s_y_ps, 1)
                    pe.wait_ge(s_y_kept, t + 2)
                    pe.wait_ge(s_gate_row, t + 1)
                    for k in range(KD):
                        pe.matmul(ps_g[:, 0:EX], yt[:, u, k, :], gw[:, k, :], start=(k == 0), stop=False)
                    pe.matmul(ps_g[:, 0:EX], m.ones[0:1, :], gb[:, :], start=False, stop=True).then_inc(s_logits, 1)
                    for q in range(QB):
                        pe.wait_ge(s_gelu, 4 * (QB * t) + 4 * max(q - 1, 0) + 1)
                        for b in range(4):
                            f = 4 * q + b
                            early = f * P < EARLY * FF
                            w1, c = (w1_first, f * P) if early else (w1_last, f * P - EARLY * FF)
                            if not early and f * P == EARLY * FF:
                                pe.wait_ge(s_w1, 16 * (EX - EARLY))
                            for k in range(KD):
                                mm = pe.matmul(ps_h[:, q % 2, b, :], w1[:, k, c:c + P], yt[:, u, k, :],
                                               start=(k == 0), stop=(k == KD - 1))
                        mm.then_inc(s_hid, 1)
                    pe.wait_ge(s_gate, t + 1)
                    pe.transpose(ps_g[0:EX, P:2 * P], g[:, 3, :], m.identf[:, :]).then_inc(s_gate_t, 1)
                    pe.wait_ge(s_gate_row, t + 2)
                    for e in range(EX):
                        mm = pe.matmul(ps_b[:, e, :], m.sel[:, e, :], gt[:, :], start=True, stop=True)
                    mm.then_inc(s_spread, 1)
                    pe.wait_ge(s_added, t + 1)
                    pe.matmul(ps_x[:, :], gt[:, :], b2[:, :], start=True, stop=False)
                    pe.wait_ge(s_w2, 32)
                    for q in range(QB):
                        pe.wait_ge(s_mixed, QB * t + q + 1)
                        for b in range(4):
                            f = 4 * q + b
                            mm = pe.matmul(ps_x[:, :], hid[:, f, :], w2[:, f, :], start=False, stop=(f == FB - 1))
                    mm.then_inc(s_out, 1)

        @block.scalar
        def _(act):
            for opened in (s_y_kept, s_gelu):
                act.sem_inc(opened, 1)
            act.wait_ge(s_small, 80)
            with act.Fori(0, NT // 2) as i:
                for u in range(2):
                    t = 2 * i + u
                    act.wait_ge(s_y_ps, t + 2)
                    act.copy(yt[:, u, :, :], ps_y[:, :, :]).then_inc(s_y_kept, 1)
                    act.wait_ge(s_step, 3 * t + 1)
                    act.activation(g[:, 0, :], ps_g[:, 0:EX], ACT.Exp, bias=g[:, 1, 0:1],
                                   accum_out=g[:, 1, 1:2]).then_inc(s_expd, 1)
                    act.wait_ge(s_out, t + 1)
                    for q in range(QB):
                        act.wait_ge(s_hid, QB * t + q + 1)
                        for b in range(4):
                            f = 4 * q + b
                            act.activation(hid[:, f, :], ps_h[:, q % 2, b, :], ACT.Gelu_apprx_tanh,
                                           bias=b1[:, f:f + 1]).then_inc(s_gelu, 1)

        @block.vector
        def _(dve):
            for opened in (s_cols, s_gate_row, s_added):
                dve.sem_inc(opened, 1)
            with dve.Fori(0, NT // 2) as i:
                for u in range(2):
                    t = 2 * i + u
                    dve.wait_ge(s_turned, t + 2)
                    dve.wait_ge(s_y_ps, 2 * i + 1)
                    dve.tensor_copy(ot[:, u, :, :], ps_t[:, :, :]).then_inc(s_cols, 1)
                    dve.wait_ge(s_logits, t + 1)
                    dve.tensor_reduce(g[:, 1, 0:1], ps_g[:, 0:EX], AX_X, ALU.max, negate=True).then_inc(s_step, 1)
                    dve.wait_ge(s_expd, t + 1)
                    dve.reciprocal(g[:, 1, 2:3], g[:, 1, 1:2]).then_inc(s_step, 1)
                    dve.wait_ge(s_step, 3 * t + 2)
                    dve.wait_ge(s_gate_t, t + 1)
                    dve.tensor_scalar(g[:, 3, :], g[:, 0, :], g[:, 1, 2:3], None, ALU.mult).then_inc(s_gate, 1)
                    dve.wait_ge(s_gate_t, t + 2)
                    dve.wait_ge(s_out, t + 1)
                    dve.tensor_copy(gt[:, :], ps_g[0:EX, P:2 * P]).then_inc(s_gate_row, 1)
                    dve.wait_ge(s_spread, t + 1)
                    for q in range(QB):
                        dve.wait_ge(s_gelu, 4 * (QB * t) + 4 * q + 4 + 1)
                        for e in range(2):
                            h2 = hid[:, 4 * q + 2 * e:4 * q + 2 * e + 2, :]
                            ins = dve.tensor_tensor(h2, h2, ps_b[:, 2 * q + e, :].unsqueeze(1).broadcast_to([P, 2, P]),
                                                    ALU.mult)
                        ins.then_inc(s_mixed, 1)
                    dve.wait_ge(s_out, t + 2)
                    x_t = m.X[:, bass.ds(t, 1), :]
                    dve.tensor_tensor(x_t, x_t, ps_x[:, :].unsqueeze(1), ALU.add).then_inc(s_added, 1)
                    dve.wait_ge(s_added, t + 2)
                    dve.bn_stats(m.stats[:, bass.ds(t, 1), :], x_t).then_inc(s_step, 1)


def conv_cols(nc, m, io, ct):
    with ExitStack() as ctx:
        s = Stage(nc, m, ctx, "cv")
        (s_small, s_rows, s_turned, s_cols, s_edge, s_mid, s_step) = s.signals(
            "small rows turned cols edge mid step")
        z = s.sb("z", [P, KD, NP + 2])
        zn = s.sb("zn", [P, 2, D])
        taps = s.sb("taps", [P, KD, 4])
        ps_t = s.psum("ps_t", [P, 2, KD, P])
        block = ctx.enter_context(nc.Block())

        @block.sync
        def _(sp):
            sp.dma_start(taps[:, :, 0:3], io["L1_ffn_pos_w"].rearrange("(k p) a c -> p k (a c)", p=P)
                         ).then_inc(s_small, 16)
            sp.dma_start(taps[:, :, 3:4], io["L1_ffn_pos_b"].rearrange("(k p a) -> p k a", p=P, a=1)
                         ).then_inc(s_small, 16)
            sp.wait_ge(s_small, 32)

        @block.tensor
        def _(pe):
            for opened in (s_turned,):
                pe.sem_inc(opened, 1)
            with pe.Fori(0, NT // 2) as i:
                for u in range(2):
                    pe.wait_ge(s_rows, 2 * i + u + 1)
                    pe.wait_ge(s_cols, 2 * i + 1)
                    for k in range(KD):
                        mm = pe.transpose(ps_t[:, u, k, :], zn[:, u, k * P:(k + 1) * P], m.identf[:, :])
                    mm.then_inc(s_turned, 1)

        @block.scalar
        def _(act):
            with act.Fori(0, NT // 2) as i:
                for u in range(2):
                    t = 2 * i + u
                    act.wait_ge(s_turned, 2 * i + 1)
                    act.activation(zn[:, u, :], m.X[:, bass.ds(t, 1), :], ACT.Identity,
                                   bias=m.shift[:, bass.ds(t, 1)], scale=m.scale[:, bass.ds(t, 1)]
                                   ).then_inc(s_rows, 1)
            act.wait_ge(s_small, 32)
            act.wait_ge(s_edge, 2)
            for k in range(KD):
                act.activation(ct[:, k, :], z[:, k, 1:NP + 1], ACT.Identity, scale=taps[:, k, 1:2],
                               bias=taps[:, k, 3:4]).then_inc(s_mid, 1)

        @block.vector
        def _(dve):
            for opened in (s_cols,):
                dve.sem_inc(opened, 1)
            with dve.Fori(0, NT // 2) as i:
                for u in range(2):
                    t = 2 * i + u
                    dve.wait_ge(s_turned, t + 2)
                    dve.tensor_copy(z[:, :, bass.ds(t * P + 1, P)], ps_t[:, u, :, :]).then_inc(s_cols, 1)
            dve.wait_ge(s_cols, NT + 1)
            dve.memset(z[:, :, 0:1], 0.0).then_inc(s_edge, 1)
            dve.memset(z[:, :, N + 1:NP + 2], 0.0).then_inc(s_edge, 1)
            dve.wait_ge(s_edge, 2)
            dve.wait_ge(s_small, 32)
            for k in range(KD):
                dve.wait_ge(s_mid, k + 1)
                for n, tap in enumerate((0, 2)):
                    dve.scalar_tensor_tensor(out=ct[:, k, :], in0=z[:, k, tap:tap + NP], scalar=taps[:, k, tap:tap + 1],
                                             in1=ct[:, k, :], op0=ALU.mult, op1=ALU.add).then_inc(s_step, 1)
                    dve.wait_ge(s_step, 3 * k + n + 1)
                dve.tensor_tensor(ct[:, k, :], ct[:, k, :], z[:, k, 1:NP + 1], ALU.add).then_inc(s_step, 1)


def top_qkv(nc, m, io, ct, wt, QO, KT, V):
    with ExitStack() as ctx:
        s = Stage(nc, m, ctx, "tq")
        (s_small, s_projected, s_kept, s_cut, s_v_ps, s_v_kept) = s.signals(
            "small projected kept cut v_ps v_kept")
        qb = s.sb("qb", [P, 2 * KD])
        cs = s.sb("cs", [P, 2, KD, P])
        ps = s.psum("ps", [P, 4, BANK])
        ps_v = s.psum("ps_v", [P, 2, BANK])
        block = ctx.enter_context(nc.Block())
        scale = float(D) ** -0.5

        @block.sync
        def _(sp):
            sp.dma_start(qb[:, :], io["L1_ffn_qkv_b"][0:2 * D].rearrange("(k p) -> p k", p=P)).then_inc(s_small, 16)
            sp.wait_ge(s_small, 16)

        @block.gpsimd
        def _(pool):
            pool.memset(V[:, :, :].rearrange("p t (h c) -> p (t h) c", h=H)[:, :, DH:DH + 1], 1.0)

        @block.tensor
        def _(pe):
            for opened in (s_v_ps,):
                pe.sem_inc(opened, 1)
            with pe.Fori(0, NCH) as c:
                for f in range(2 * KD):
                    pe.wait_ge(s_kept, 2 * KD * c + max(f - 3, 0) + 1)
                    for k in range(KD):
                        mm = pe.matmul(ps[:, f % 4, 0:CH], wt[:, k, f * P:(f + 1) * P], ct[:, k, bass.ts(c, CH)],
                                       start=(k == 0), stop=(k == KD - 1))
                    mm.then_inc(s_projected, 1)
            with pe.Fori(0, NT // 2) as i:
                for u in range(2):
                    t = 2 * i + u
                    pe.wait_ge(s_cut, t + 1)
                    pe.wait_ge(s_v_kept, 2 * i + 1)
                    for k in range(KD):
                        mm = pe.matmul(ps_v[:, u, :], cs[:, u, k, :], wt[:, k, 2 * D:3 * D],
                                       start=(k == 0), stop=(k == KD - 1))
                    mm.then_inc(s_v_ps, 1)

        @block.scalar
        def _(act):
            with act.Fori(0, NT // 2) as i:
                for u in range(2):
                    t = 2 * i + u
                    act.wait_ge(s_v_ps, 2 * i + 1)
                    act.copy(cs[:, u, :, :], ct[:, :, bass.ts(t, P)]).then_inc(s_cut, 1)

        @block.vector
        def _(dve):
            for opened in (s_kept, s_v_kept):
                dve.sem_inc(opened, 1)
            dve.wait_ge(s_small, 16)
            with dve.Fori(0, NCH) as c:
                for f in range(2 * KD):
                    dve.wait_ge(s_projected, 2 * KD * c + f + 1)
                    out = (QO if f < KD else KT)[:, f % KD, bass.ts(c, CH)]
                    dve.tensor_scalar(out, ps[:, f % 4, 0:CH], qb[:, f:f + 1], scale if f < KD else 1.0,
                                      ALU.add, ALU.mult).then_inc(s_kept, 1)
            with dve.Fori(0, NT // 2) as i:
                for u in range(2):
                    t = 2 * i + u
                    dve.wait_ge(s_v_ps, t + 2)
                    dve.tensor_tensor(V[:, bass.ds(t, 1), :].rearrange("p t (h c) -> p (t h) c", h=H)[:, :, 0:DH],
                                      ps_v[:, u, :].rearrange("p (h c) -> p h c", h=H),
                                      m.v_b[:, :].rearrange("p (h c) -> p h c", h=H), ALU.add
                                      ).then_inc(s_v_kept, 1)


def project_out(nc, m, QO, wo, out):
    with ExitStack() as ctx:
        s = Stage(nc, m, ctx, "po")
        (s_rows, s_turned, s_cols, s_ps, s_step, s_final, s_stored) = s.signals(
            "rows turned cols ps step final stored")
        os_ = s.sb("os_", [P, 2, KD, P])
        ot = s.sb("ot", [P, 2, KD, P])
        ps_t = s.psum("ps_t", [P, 2, KD, P])
        ps_x = s.psum("ps_x", [P, 2, BANK])
        block = ctx.enter_context(nc.Block())

        @block.gpsimd
        def _(pool):
            with pool.Fori(0, NT // 2) as i:
                for u in range(2):
                    pool.wait_ge(s_turned, 2 * i + 1)
                    pool.tensor_copy(os_[:, u, :, :], QO[:, :, bass.ts(2 * i + u, P)]).then_inc(s_rows, 1)

        @block.tensor
        def _(pe):
            for opened in (s_turned, s_ps):
                pe.sem_inc(opened, 1)
            with pe.Fori(0, NT // 2) as i:
                for u in range(2):
                    t = 2 * i + u
                    pe.wait_ge(s_rows, t + 1)
                    pe.wait_ge(s_cols, 2 * i + 1)
                    for k in range(KD):
                        mm = pe.transpose(ps_t[:, u, k, :], os_[:, u, k, :], m.identf[:, :])
                    mm.then_inc(s_turned, 1)
                    pe.wait_ge(s_cols, t + 2)
                    pe.wait_ge(s_final, 2 * i + 1)
                    for k in range(KD):
                        mm = pe.matmul(ps_x[:, u, :], ot[:, u, k, :], wo[:, k, :], start=(k == 0), stop=(k == KD - 1))
                    mm.then_inc(s_ps, 1)

        @block.vector
        def _(dve):
            for opened in (s_cols, s_final):
                dve.sem_inc(opened, 1)
            with dve.Fori(0, NT // 2) as i:
                for u in range(2):
                    t = 2 * i + u
                    x_t = m.X[:, bass.ds(t, 1), :]
                    dve.wait_ge(s_turned, t + 2)
                    dve.wait_ge(s_ps, 2 * i + 1)
                    dve.tensor_copy(ot[:, u, :, :], ps_t[:, u, :, :]).then_inc(s_cols, 1)
                    dve.tensor_tensor(x_t, x_t, m.wo_b[:, :].unsqueeze(1), ALU.add).then_inc(s_step, 1)
                    dve.wait_ge(s_step, t + 1)
                    dve.wait_ge(s_ps, t + 2)
                    dve.tensor_tensor(x_t, x_t, ps_x[:, u:u + 1, :], ALU.add).then_inc(s_final, 1)

        @block.sync
        def _(sp):
            for t in range(NT):
                rows = P if t < NT - 1 else TAIL
                sp.wait_ge(s_final, t + 2)
                sp.dma_start(out[t * P:t * P + rows, :], m.X[0:rows, t, :]).then_inc(s_stored, 16)
            sp.wait_ge(s_stored, 16 * NT)


def load(nc, name, pairs):
    with ExitStack() as ctx:
        done = ctx.enter_context(nc.semaphore(f"{name}_loaded"))
        block = ctx.enter_context(nc.Block())

        @block.sync
        def _(sp):
            for dst, src in pairs:
                sp.dma_start(dst, src).then_inc(done, 16)
            sp.wait_ge(done, 16 * len(pairs))


def rows_of(w):
    return w.rearrange("(k p) n -> p k n", p=P)


class Memory:

    def __init__(self, nc, ctx):
        def sb(name, shape, dt=F32):
            return ctx.enter_context(nc.sbuf_tensor(name, shape, dt))

        self.stages = 0
        self.X = sb("X", [P, NT, D])
        self.AT = sb("AT", [P, NT, NP], F16)
        self.identf = sb("identf", [P, P])
        self.ident16 = sb("ident16", [P, P], F16)
        self.ruler = sb("ruler", [P, NP], F16)
        self.causal = sb("causal", [P, P])
        self.ones = sb("ones", [P, P])
        self.sel = sb("sel", [EX, EX, P])
        self.padded = sb("padded", [P, NT])
        self.eps = sb("eps", [P, 2])
        self.stats = sb("stats", [P, NT, 6])
        self.mv = sb("mv", [P, NT, 2])
        self.scale = sb("scale", [P, NT])
        self.shift = sb("shift", [P, NT])
        self.deg_s = sb("deg_s", [P, NT])
        self.deg_d = sb("deg_d", [P, NT])
        self.bias0, self.bias1, self.gamma1, self.beta1, self.wo_b, self.v_b = (
            sb(name, [P, D]) for name in ("bias0", "bias1", "gamma1", "beta1", "wo_b", "v_b"))


def build(nc, io, out):
    with ExitStack() as whole, nc.allow_non_contiguous_dma(reason="vectors of a few hundred elements"):
        m = Memory(nc, whole)
        load_consts(nc, m, io)
        with ExitStack() as ctx:
            m.A = ctx.enter_context(nc.sbuf_tensor("A", [P, NT, NP], F16))
            wc = ctx.enter_context(nc.sbuf_tensor("wc", [P, KD, D], F32))
            wn = ctx.enter_context(nc.sbuf_tensor("wn", [P, KD, D], F32))
            w_in = ctx.enter_context(nc.semaphore("g0_in"))
            count_edges(nc, m, io, (w_in, [(wc[:, :, :], rows_of(io["L0_gnn_wc"])),
                                           (wn[:, :, :], rows_of(io["L0_gnn_wn"]))]))
            graph_layer(nc, m, m.A, m.deg_s, wc, wn, m.bias0)
        with ExitStack() as ctx:
            QO = ctx.enter_context(nc.sbuf_tensor("QO", [P, KD, NP], F32))
            w1_first = ctx.enter_context(nc.sbuf_tensor("w1_first", [P, KD, EARLY * FF], F32))
            w1_in = ctx.enter_context(nc.semaphore("w1_in"))
            with ExitStack() as att:
                KT = att.enter_context(nc.sbuf_tensor("KT", [P, KD, NP], F32))
                V = att.enter_context(nc.sbuf_tensor("V", [P, NT, H * (DH + 1)], F32))
                norm_scales(nc, m, twice=True)
                causal_qkv(nc, m, io, QO, KT, V)
                attention(nc, m, QO, KT, V, top=False, ahead=(w1_in, [
                    (w1_first[:, :, e * FF:(e + 1) * FF], rows_of(io["L0_ffn_W1"][e])) for e in range(EARLY)]))
            w1_last = ctx.enter_context(nc.sbuf_tensor("w1_last", [P, KD, (EX - EARLY) * FF], F32))
            w2 = ctx.enter_context(nc.sbuf_tensor("w2", [P, FB, D], F32))
            experts(nc, m, io, QO, w1_first, w1_last, w2)
        with ExitStack() as ctx:
            raw = ctx.enter_context(nc.sbuf_tensor("raw_g", [P, 2, KD, D], F32))
            ws = ctx.enter_context(nc.sbuf_tensor("ws", [P, KD, D], F32))
            wn = ctx.enter_context(nc.sbuf_tensor("wn1", [P, KD, D], F32))
            load(nc, "g1", [(raw[:, 0, :, :], rows_of(io["L1_gnn_W_self"])),
                            (raw[:, 1, :, :], rows_of(io["L1_gnn_W_neigh"]))])
            turn_weights(nc, m, [raw[:, 0, :, :], raw[:, 1, :, :]], [ws, wn])
            graph_layer(nc, m, m.AT, m.deg_d, ws, wn, m.bias1, affine=(m.gamma1, m.beta1))
        with ExitStack() as ctx:
            QO = ctx.enter_context(nc.sbuf_tensor("QO1", [P, KD, NP], F32))
            KT = ctx.enter_context(nc.sbuf_tensor("KT1", [P, KD, NP], F32))
            V = ctx.enter_context(nc.sbuf_tensor("V1", [P, NT, H * (DH + 1)], F32))
            wo = ctx.enter_context(nc.sbuf_tensor("wo1", [P, KD, D], F32))
            norm_scales(nc, m)
            with ExitStack() as pre:
                wt = pre.enter_context(nc.sbuf_tensor("wt", [P, KD, 3 * D], F32))
                with ExitStack() as r:
                    raw = r.enter_context(nc.sbuf_tensor("raw_q", [P, 4 * KD, D], F32))
                    load(nc, "f1", [(raw[:, 0:3 * KD, :], rows_of(io["L1_ffn_qkv_w"])),
                                    (raw[:, 3 * KD:4 * KD, :], rows_of(io["L1_ffn_wo_w"]))])
                    turn_weights(nc, m, [raw[:, 0:3 * KD, :], raw[:, 3 * KD:4 * KD, :]], [wt, wo])
                ct = pre.enter_context(nc.sbuf_tensor("ct", [P, KD, NP], F32))
                conv_cols(nc, m, io, ct)
                top_qkv(nc, m, io, ct, wt, QO, KT, V)
            attention(nc, m, QO, KT, V, top=True)
            project_out(nc, m, QO, wo, out)


def graph_layer(nc, m, adj, deg, w_own, w_near, bias, affine=None):
    with ExitStack() as ctx:
        s = Stage(nc, m, ctx, "gl")
        xn = s.sb("xn", [P, NT, D])
        agg = s.sb("agg", [P, KD, NP])
        norm_scales(nc, m)
        with ExitStack() as parts:
            p = Stage(nc, m, parts, "gp")
            hi = p.sb("hi", [P, NT, D], F16)
            lo = p.sb("lo", [P, NT, D], F16)
            node_rows(nc, m, xn, hi, lo)
            aggregate(nc, m, hi, lo, adj, agg)
        graph_rows(nc, m, xn, agg, w_own, w_near, deg, bias, affine)


_INS = ["x", "src", "dst", "L0_gnn_wc", "L0_gnn_wn", "L0_gnn_bias", "L0_ffn_ln_g", "L0_ffn_ln_b", "L0_ffn_Wq",
        "L0_ffn_Wk", "L0_ffn_Wv", "L0_ffn_Wo", "L0_ffn_qn_g", "L0_ffn_kn_g", "L0_ffn_gate_W", "L0_ffn_gate_b",
        "L0_ffn_W1", "L0_ffn_b1", "L0_ffn_W2", "L0_ffn_b2", "L1_gnn_W_self", "L1_gnn_W_neigh", "L1_gnn_bias",
        "L1_gnn_gamma", "L1_gnn_beta", "L1_ffn_pos_w", "L1_ffn_pos_b", "L1_ffn_qkv_w", "L1_ffn_qkv_b",
        "L1_ffn_wo_w", "L1_ffn_wo_b"]


def kernel(**inputs):
    import numpy as np
    from concourse import bacc
    from concourse.bass_utils import run_bass_kernel_spmd

    nc = bacc.Bacc("TRN2", target_bir_lowering=False, num_devices=1)
    arrays, io = {}, {}
    for name in _INS:
        a = np.ascontiguousarray(inputs[name])
        arrays[f"in_{name}"] = a
        io[name] = nc.dram_tensor(f"in_{name}", a.shape, mybir.dt.from_np(a.dtype), kind="ExternalInput").ap()
    out = nc.dram_tensor("out_x", (N, D), F32, kind="ExternalOutput").ap()
    build(nc, io, out)
    r = run_bass_kernel_spmd(nc, [arrays], core_ids=[0])
    return r.results[0]["out_x"]
```
